# Optimizing a Trainium2 kernel written in Bass

```python
import numpy as np
import jax
import jax.numpy as jnp

def _softmax(x, axis=-1):
    return jax.nn.softmax(x, axis=axis)

def _gelu(x):
    return jax.nn.gelu(x, approximate=True)

def _silu(x):
    return jax.nn.silu(x)

def _sigmoid(x):
    return jax.nn.sigmoid(x)

def _layernorm(x, axis=-1, eps=1e-05):
    m = jnp.mean(x, axis=axis, keepdims=True)
    v = jnp.var(x, axis=axis, keepdims=True)
    return (x - m) / jnp.sqrt(v + eps)

def _scatter_add(tgt, idx, src, axis=0):
    return tgt.at[idx].add(src)

def _segment_sum(src, seg, n):
    return jax.ops.segment_sum(src, seg, n)
kernel_name = 'mk_xattn_seq_d4_seqx_r4_c096bc'

def setup_inputs(seed: int=0):
    np.random.seed(seed)
    _w = jnp.asarray

    def _rec_inputs():
        import jax
        import jax.numpy as jnp
        _rk = jax.random.key(seed)
        x = 7.22e-05 + 1 * jax.random.normal(jax.random.fold_in(_rk, 1), (4, 1024, 256), jnp.float32)
        _lenS = 1024 - jax.random.randint(jax.random.fold_in(_rk, 7), (4,), 0, max(1, 1024 // 4) + 1, jnp.int32)
        _lenS2 = 77 - jax.random.randint(jax.random.fold_in(_rk, 8), (4,), 0, max(1, 77 // 4) + 1, jnp.int32)
        _ctx_1024P = jax.random.normal(jax.random.fold_in(_rk, 11), (4, 16, 256), jnp.float32)
        _ctx_1024c = jax.random.dirichlet(jax.random.fold_in(_rk, 511), 0.3 * jnp.ones((16,), jnp.float32), (4, 77))
        _ctx_1024t = jnp.einsum('bsk,bkd->bsd', _ctx_1024c, _ctx_1024P)
        _ctx_1024t = _ctx_1024t * jax.lax.rsqrt(jnp.mean(jnp.square(_ctx_1024t)) + 1e-12) * 0.953939
        ctx_1024 = 4.13588e-05 + 0.999923 * (_ctx_1024t + 0.3 * jax.random.normal(jax.random.fold_in(_rk, 611), (4, 77, 256), jnp.float32))
        itok_BxS2_4_31999 = jax.random.randint(jax.random.fold_in(_rk, 12), (4, 77), 4, 8000, jnp.int32)
        _ctxb_2048x64P = jax.random.normal(jax.random.fold_in(_rk, 13), (4, 16, 64), jnp.float32)
        _ctxb_2048x64c = jax.random.dirichlet(jax.random.fold_in(_rk, 513), 0.3 * jnp.ones((16,), jnp.float32), (4, 77))
        _ctxb_2048x64t = jnp.einsum('bsk,bkd->bsd', _ctxb_2048x64c, _ctxb_2048x64P)
        _ctxb_2048x64t = _ctxb_2048x64t * jax.lax.rsqrt(jnp.mean(jnp.square(_ctxb_2048x64t)) + 1e-12) * 0.953939
        ctxb_2048x64 = 0.50053 + 0.288505 * (_ctxb_2048x64t + 0.3 * jax.random.normal(jax.random.fold_in(_rk, 613), (4, 77, 64), jnp.float32))
        _validS = jnp.arange(1024)[None, :] < _lenS[:, None]
        _validS2 = jnp.arange(77)[None, :] < _lenS2[:, None]
        _causal = jnp.tril(jnp.ones((1024, 1024), dtype=bool))
        mask_1x1xSxS2_if1 = jnp.where(jnp.ones((1, 1, 1024, 77), dtype=bool), 1, 0).astype(jnp.int32)
        mask_BxSxS2_bk0 = jnp.logical_not(jnp.broadcast_to(_validS2[:, None, :], (4, 1024, 77)))
        return (x, ctx_1024, itok_BxS2_4_31999, ctxb_2048x64, mask_1x1xSxS2_if1, mask_BxSxS2_bk0)
    x, ctx_1024, itok_BxS2_4_31999, ctxb_2048x64, mask_1x1xSxS2_if1, mask_BxSxS2_bk0 = _rec_inputs()

    def _L0_xattn_setup():
        import jax, jax.numpy as jnp
        import numpy as np
        BATCH, T, H, S, P, NH = (4, 512, 256, 64, 64, 8)
        HD = H // NH

        def _layernorm(x, g, b):
            mu = jnp.mean(x, axis=-1, keepdims=True)
            var = jnp.mean((x - mu) ** 2, axis=-1, keepdims=True)
            return (x - mu) * jax.lax.rsqrt(var + 1e-05) * g + b

        def _mha(q_in, kv_in, W_qkv, b_qkv, W_o, b_o):
            Wq, Wk, Wv = jnp.split(W_qkv, 3, axis=0)
            bq, bk, bv = jnp.split(b_qkv, 3, axis=0)

            def heads(x, W, b):
                y = x @ W.T + b
                return y.reshape(y.shape[0], y.shape[1], NH, HD).transpose(0, 2, 1, 3)
            q, k, v = (heads(q_in, Wq, bq), heads(kv_in, Wk, bk), heads(kv_in, Wv, bv))
            scores = jnp.einsum('bhqd,bhkd->bhqk', q, k) * (1.0 / np.sqrt(HD))
            attn = jax.nn.softmax(scores, axis=-1)
            out = jnp.einsum('bhqk,bhkd->bhqd', attn, v)
            out = out.transpose(0, 2, 1, 3).reshape(q_in.shape)
            return out @ W_o.T + b_o
        key = jax.random.key(seed)
        ks = jax.random.split(key, 16)
        sH = 1.0 / np.sqrt(H)
        d = {}
        d['builder_state'] = jax.random.normal(ks[0], (BATCH, T, H), jnp.float32)
        d['base_state'] = jax.random.normal(ks[1], (BATCH, T, H), jnp.float32)
        d['input_ids'] = jax.random.randint(ks[2], (BATCH, T), 0, 8000)
        d['program_probs'] = jax.random.uniform(ks[3], (BATCH, T, P), jnp.float32)
        d['A'] = jax.random.normal(ks[4], (S, S), jnp.float32) * (0.5 / np.sqrt(S))
        d['Bmat'] = jax.random.normal(ks[5], (H, S), jnp.float32) * sH
        d['Cmat'] = jax.random.normal(ks[6], (S, H), jnp.float32) * (1.0 / np.sqrt(S))
        d['W_in'] = jax.random.normal(ks[7], (H, H), jnp.float32) * sH
        d['b_in'] = jnp.zeros((H,), jnp.float32)
        d['W_qkv'] = jax.random.normal(ks[8], (3 * H, H), jnp.float32) * sH
        d['b_qkv'] = jnp.zeros((3 * H,), jnp.float32)
        d['W_o'] = jax.random.normal(ks[9], (H, H), jnp.float32) * sH
        d['b_o'] = jnp.zeros((H,), jnp.float32)
        d['W_prog'] = jax.random.normal(ks[10], (H, P), jnp.float32) * (1.0 / np.sqrt(P))
        d['b_prog'] = jnp.zeros((H,), jnp.float32)
        d['g1'] = jnp.ones((H,), jnp.float32)
        d['beta1'] = jnp.zeros((H,), jnp.float32)
        d['g2'] = jnp.ones((H,), jnp.float32)
        d['beta2'] = jnp.zeros((H,), jnp.float32)
        return d
    _L0_xattn_all = _L0_xattn_setup()
    _L0_xattn_in = {k: v for k, v in _L0_xattn_all.items() if k in ('A', 'Bmat', 'Cmat', 'W_in', 'b_in', 'W_qkv', 'b_qkv', 'W_o', 'b_o', 'W_prog', 'b_prog', 'g1', 'beta1', 'g2', 'beta2')}
    del _L0_xattn_all

    def _L1_xattn_setup():
        import jax, jax.numpy as jnp
        import numpy as np
        B, T, E = (4, 512, 256)
        H, HS = (16, 64)
        EPS = 1e-05

        def _layernorm(x, g, b):
            mu = jnp.mean(x, axis=-1, keepdims=True)
            var = jnp.mean(jnp.square(x - mu), axis=-1, keepdims=True)
            return (x - mu) * jax.lax.rsqrt(var + EPS) * g + b
        key = jax.random.key(seed)
        ks = jax.random.split(key, 8)
        q = jax.random.normal(ks[0], (B, T, E), dtype=jnp.float32)
        s_in = 1.0 / np.sqrt(E)
        s_o = 1.0 / np.sqrt(H * HS)
        return {'q': q, 'kv': q, 'ln_g': jnp.ones((E,), jnp.float32), 'ln_b': jnp.zeros((E,), jnp.float32), 'wq': jax.random.uniform(ks[1], (E, H * HS), jnp.float32, -s_in, s_in), 'bq': jax.random.uniform(ks[2], (H * HS,), jnp.float32, -s_in, s_in), 'wkv': jax.random.uniform(ks[3], (E, 2 * H * HS), jnp.float32, -s_in, s_in), 'bkv': jax.random.uniform(ks[4], (2 * H * HS,), jnp.float32, -s_in, s_in), 'wo': jax.random.uniform(ks[5], (H * HS, E), jnp.float32, -s_o, s_o), 'bo': jax.random.uniform(ks[6], (E,), jnp.float32, -s_o, s_o)}
    _L1_xattn_all = _L1_xattn_setup()
    _L1_xattn_in = {k: v for k, v in _L1_xattn_all.items() if k in ('ln_g', 'ln_b', 'wq', 'bq', 'wkv', 'bkv', 'wo', 'bo')}
    del _L1_xattn_all

    def _L2_xattn_setup():
        import jax, jax.numpy as jnp
        import numpy as np
        B, S, D, H = (4, 512, 256, 16)
        DK = D // H

        def _split_heads(x):
            b, s, _ = x.shape
            return x.reshape(b, s, H, DK).transpose(0, 2, 1, 3)
        key = jax.random.key(seed)
        ks = jax.random.split(key, 12)

        def xavier(k, shape):
            fan_in, fan_out = (shape[1], shape[0])
            limit = (6.0 / (fan_in + fan_out)) ** 0.5
            return jax.random.uniform(k, shape, jnp.float32, -limit, limit)
        inp = {'q': jax.random.normal(ks[0], (B, S, D), jnp.float32), 'k': jax.random.normal(ks[1], (B, S, D), jnp.float32), 'v': jax.random.normal(ks[2], (B, S, D), jnp.float32), 'mask': jnp.ones((1, 1, S, S), jnp.int32), 'Wq': xavier(ks[3], (D, D)), 'bq': jnp.zeros((D,), jnp.float32), 'Wk': xavier(ks[4], (D, D)), 'bk': jnp.zeros((D,), jnp.float32), 'Wv': xavier(ks[5], (D, D)), 'bv': jnp.zeros((D,), jnp.float32), 'Wo': xavier(ks[6], (D, D)), 'bo': jnp.zeros((D,), jnp.float32), 'ln_g': jnp.ones((D,), jnp.float32), 'ln_b': jnp.zeros((D,), jnp.float32)}
        return inp
    _L2_xattn_all = _L2_xattn_setup()
    _L2_xattn_in = {k: v for k, v in _L2_xattn_all.items() if k in ('Wq', 'bq', 'Wk', 'bk', 'Wv', 'bv', 'Wo', 'bo', 'ln_g', 'ln_b')}
    del _L2_xattn_all

    def _L3_xattn_setup():
        import jax, jax.numpy as jnp
        import numpy as np
        EPS = 1e-05

        def layer_norm(x, w, b):
            mu = jnp.mean(x, axis=-1, keepdims=True)
            var = jnp.var(x, axis=-1, keepdims=True)
            return (x - mu) * jax.lax.rsqrt(var + EPS) * w + b
        key = jax.random.key(seed)
        ks = jax.random.split(key, 12)
        B, N, M, C = (2, 512, 512, 256)
        H = 16
        hid = 4 * C
        s = lambda d: 1.0 / np.sqrt(d)
        return {'x': jax.random.normal(ks[0], (B, N, C), jnp.float32), 'context': jax.random.normal(ks[1], (B, M, C), jnp.float32), 'xa_mask': jax.random.bernoulli(ks[2], 0.1, (B, N, M)), 'qn_w': jnp.ones((C,), jnp.float32), 'qn_b': jnp.zeros((C,), jnp.float32), 'cn_w': jnp.ones((C,), jnp.float32), 'cn_b': jnp.zeros((C,), jnp.float32), 'n2_w': jnp.ones((C,), jnp.float32), 'n2_b': jnp.zeros((C,), jnp.float32), 'q_w': jax.random.normal(ks[3], (C, C), jnp.float32) * s(C), 'kv_w': jax.random.normal(ks[4], (C, 2 * C), jnp.float32) * s(C), 'proj_w': jax.random.normal(ks[5], (C, C), jnp.float32) * s(C), 'proj_b': jnp.zeros((C,), jnp.float32), 'fc1_w': jax.random.normal(ks[6], (C, hid), jnp.float32) * s(C), 'fc1_b': jnp.zeros((hid,), jnp.float32), 'fc2_w': jax.random.normal(ks[7], (hid, C), jnp.float32) * s(hid), 'fc2_b': jnp.zeros((C,), jnp.float32)}
    _L3_xattn_all = _L3_xattn_setup()
    _L3_xattn_in = {k: v for k, v in _L3_xattn_all.items() if k in ('qn_w', 'qn_b', 'cn_w', 'cn_b', 'n2_w', 'n2_b', 'q_w', 'kv_w', 'proj_w', 'proj_b', 'fc1_w', 'fc1_b', 'fc2_w', 'fc2_b')}
    del _L3_xattn_all
    return {'x': x, 'ctx_1024': ctx_1024, 'itok_BxS2_4_31999': itok_BxS2_4_31999, 'ctxb_2048x64': ctxb_2048x64, 'mask_1x1xSxS2_if1': mask_1x1xSxS2_if1, 'mask_BxSxS2_bk0': mask_BxSxS2_bk0, 'L0_xattn_A': _L0_xattn_in['A'], 'L0_xattn_Bmat': _L0_xattn_in['Bmat'], 'L0_xattn_Cmat': _L0_xattn_in['Cmat'], 'L0_xattn_W_in': _L0_xattn_in['W_in'], 'L0_xattn_b_in': _L0_xattn_in['b_in'], 'L0_xattn_W_qkv': _L0_xattn_in['W_qkv'], 'L0_xattn_b_qkv': _L0_xattn_in['b_qkv'], 'L0_xattn_W_o': _L0_xattn_in['W_o'], 'L0_xattn_b_o': _L0_xattn_in['b_o'], 'L0_xattn_W_prog': _L0_xattn_in['W_prog'], 'L0_xattn_b_prog': _L0_xattn_in['b_prog'], 'L0_xattn_g1': _L0_xattn_in['g1'], 'L0_xattn_beta1': _L0_xattn_in['beta1'], 'L0_xattn_g2': _L0_xattn_in['g2'], 'L0_xattn_beta2': _L0_xattn_in['beta2'], 'L1_xattn_ln_g': _L1_xattn_in['ln_g'], 'L1_xattn_ln_b': _L1_xattn_in['ln_b'], 'L1_xattn_wq': _L1_xattn_in['wq'], 'L1_xattn_bq': _L1_xattn_in['bq'], 'L1_xattn_wkv': _L1_xattn_in['wkv'], 'L1_xattn_bkv': _L1_xattn_in['bkv'], 'L1_xattn_wo': _L1_xattn_in['wo'], 'L1_xattn_bo': _L1_xattn_in['bo'], 'L2_xattn_Wq': _L2_xattn_in['Wq'], 'L2_xattn_bq': _L2_xattn_in['bq'], 'L2_xattn_Wk': _L2_xattn_in['Wk'], 'L2_xattn_bk': _L2_xattn_in['bk'], 'L2_xattn_Wv': _L2_xattn_in['Wv'], 'L2_xattn_bv': _L2_xattn_in['bv'], 'L2_xattn_Wo': _L2_xattn_in['Wo'], 'L2_xattn_bo': _L2_xattn_in['bo'], 'L2_xattn_ln_g': _L2_xattn_in['ln_g'], 'L2_xattn_ln_b': _L2_xattn_in['ln_b'], 'L3_xattn_qn_w': _L3_xattn_in['qn_w'], 'L3_xattn_qn_b': _L3_xattn_in['qn_b'], 'L3_xattn_cn_w': _L3_xattn_in['cn_w'], 'L3_xattn_cn_b': _L3_xattn_in['cn_b'], 'L3_xattn_n2_w': _L3_xattn_in['n2_w'], 'L3_xattn_n2_b': _L3_xattn_in['n2_b'], 'L3_xattn_q_w': _L3_xattn_in['q_w'], 'L3_xattn_kv_w': _L3_xattn_in['kv_w'], 'L3_xattn_proj_w': _L3_xattn_in['proj_w'], 'L3_xattn_proj_b': _L3_xattn_in['proj_b'], 'L3_xattn_fc1_w': _L3_xattn_in['fc1_w'], 'L3_xattn_fc1_b': _L3_xattn_in['fc1_b'], 'L3_xattn_fc2_w': _L3_xattn_in['fc2_w'], 'L3_xattn_fc2_b': _L3_xattn_in['fc2_b']}

def reference(x, ctx_1024, itok_BxS2_4_31999, ctxb_2048x64, mask_1x1xSxS2_if1, mask_BxSxS2_bk0, L0_xattn_A, L0_xattn_Bmat, L0_xattn_Cmat, L0_xattn_W_in, L0_xattn_b_in, L0_xattn_W_qkv, L0_xattn_b_qkv, L0_xattn_W_o, L0_xattn_b_o, L0_xattn_W_prog, L0_xattn_b_prog, L0_xattn_g1, L0_xattn_beta1, L0_xattn_g2, L0_xattn_beta2, L1_xattn_ln_g, L1_xattn_ln_b, L1_xattn_wq, L1_xattn_bq, L1_xattn_wkv, L1_xattn_bkv, L1_xattn_wo, L1_xattn_bo, L2_xattn_Wq, L2_xattn_bq, L2_xattn_Wk, L2_xattn_bk, L2_xattn_Wv, L2_xattn_bv, L2_xattn_Wo, L2_xattn_bo, L2_xattn_ln_g, L2_xattn_ln_b, L3_xattn_qn_w, L3_xattn_qn_b, L3_xattn_cn_w, L3_xattn_cn_b, L3_xattn_n2_w, L3_xattn_n2_b, L3_xattn_q_w, L3_xattn_kv_w, L3_xattn_proj_w, L3_xattn_proj_b, L3_xattn_fc1_w, L3_xattn_fc1_b, L3_xattn_fc2_w, L3_xattn_fc2_b):
    import jax
    import jax.numpy as jnp

    def _L0_xattn_ref(builder_state, base_state, input_ids, program_probs, A, Bmat, Cmat, W_in, b_in, W_qkv, b_qkv, W_o, b_o, W_prog, b_prog, g1, beta1, g2, beta2):
        import jax, jax.numpy as jnp
        import numpy as np
        BATCH, T, H, S, P, NH = (4, 512, 256, 64, 64, 8)
        HD = H // NH

        def _layernorm(x, g, b):
            mu = jnp.mean(x, axis=-1, keepdims=True)
            var = jnp.mean((x - mu) ** 2, axis=-1, keepdims=True)
            return (x - mu) * jax.lax.rsqrt(var + 1e-05) * g + b

        def _mha(q_in, kv_in, W_qkv, b_qkv, W_o, b_o):
            Wq, Wk, Wv = jnp.split(W_qkv, 3, axis=0)
            bq, bk, bv = jnp.split(b_qkv, 3, axis=0)

            def heads(x, W, b):
                y = x @ W.T + b
                return y.reshape(y.shape[0], y.shape[1], NH, HD).transpose(0, 2, 1, 3)
            q, k, v = (heads(q_in, Wq, bq), heads(kv_in, Wk, bk), heads(kv_in, Wv, bv))
            scores = jnp.einsum('bhqd,bhkd->bhqk', q, k) * (1.0 / np.sqrt(HD))
            attn = jax.nn.softmax(scores, axis=-1)
            out = jnp.einsum('bhqk,bhkd->bhqd', attn, v)
            out = out.transpose(0, 2, 1, 3).reshape(q_in.shape)
            return out @ W_o.T + b_o
        residual = builder_state
        x = _layernorm(builder_state, g1, beta1)
        base_n = _layernorm(base_state, g1, beta1)
        x = residual + _mha(x, base_n, W_qkv, b_qkv, W_o, b_o)
        residual = x
        xn = _layernorm(x, g2, beta2)
        U = (xn @ W_in.T + b_in) @ Bmat

        def step(s, u_t):
            s = jax.nn.silu(s @ A.T) + u_t
            return (s, s)
        _, states = jax.lax.scan(step, jnp.zeros((builder_state.shape[0], S), U.dtype), U.transpose(1, 0, 2))
        ssm_out = jnp.einsum('tbs,sh->bth', states, Cmat)
        x = residual + ssm_out
        mod = program_probs.mean(axis=1) @ W_prog.T + b_prog
        return x + mod[:, None, :]

    def _L1_xattn_ref(q, kv, ln_g, ln_b, wq, bq, wkv, bkv, wo, bo):
        import jax, jax.numpy as jnp
        import numpy as np
        B, T, E = (4, 512, 256)
        H, HS = (16, 64)
        EPS = 1e-05

        def _layernorm(x, g, b):
            mu = jnp.mean(x, axis=-1, keepdims=True)
            var = jnp.mean(jnp.square(x - mu), axis=-1, keepdims=True)
            return (x - mu) * jax.lax.rsqrt(var + EPS) * g + b
        oq = q
        qn = _layernorm(q, ln_g, ln_b)
        kvn = _layernorm(kv, ln_g, ln_b)
        b, qT, _ = q.shape
        kvT = kv.shape[1]
        qp = (qn @ wq + bq).reshape(b, qT, H, HS).transpose(0, 2, 1, 3)
        kvp = kvn @ wkv + bkv
        kp, vp = jnp.split(kvp, 2, axis=-1)
        kp = kp.reshape(b, kvT, H, HS).transpose(0, 2, 1, 3)
        vp = vp.reshape(b, kvT, H, HS).transpose(0, 2, 1, 3)
        attn = jnp.einsum('bhqd,bhkd->bhqk', qp, kp) / jnp.sqrt(jnp.float32(HS))
        causal = jnp.tril(jnp.ones((qT, kvT), dtype=bool))
        attn = jnp.where(causal, attn, -jnp.inf)
        attn = jax.nn.softmax(attn, axis=-1)
        ctx = jnp.einsum('bhqk,bhkd->bhqd', attn, vp)
        ctx = ctx.transpose(0, 2, 1, 3).reshape(b, qT, H * HS)
        out = ctx @ wo + bo + oq
        return out

    def _L2_xattn_ref(q, k, v, mask, Wq, bq, Wk, bk, Wv, bv, Wo, bo, ln_g, ln_b):
        import jax, jax.numpy as jnp
        import numpy as np
        B, S, D, H = (4, 512, 256, 16)
        DK = D // H

        def _split_heads(x):
            b, s, _ = x.shape
            return x.reshape(b, s, H, DK).transpose(0, 2, 1, 3)
        residual = q
        qh = _split_heads(q @ Wq.T + bq)
        kh = _split_heads(k @ Wk.T + bk)
        vh = _split_heads(v @ Wv.T + bv)
        scale = jnp.sqrt(jnp.asarray(DK, qh.dtype))
        scores = jnp.einsum('bhqd,bhkd->bhqk', qh, kh) / scale
        scores = jnp.where(mask == 0, jnp.asarray(-1000000000.0, scores.dtype), scores)
        m = jnp.max(scores, axis=-1, keepdims=True)
        e = jnp.exp(scores - m) * mask.astype(scores.dtype)
        probs = e / (jnp.sum(e, axis=-1, keepdims=True) + 1e-09)
        attn = jnp.einsum('bhqk,bhkd->bhqd', probs, vh)
        attn = attn.transpose(0, 2, 1, 3).reshape(q.shape[0], -1, D)
        out = attn @ Wo.T + bo
        x = out + residual
        mu = jnp.mean(x, axis=-1, keepdims=True)
        var = jnp.mean((x - mu) ** 2, axis=-1, keepdims=True)
        return (x - mu) / jnp.sqrt(var + 1e-05) * ln_g + ln_b

    def _L3_xattn_ref(x, context, xa_mask, qn_w, qn_b, cn_w, cn_b, n2_w, n2_b, q_w, kv_w, proj_w, proj_b, fc1_w, fc1_b, fc2_w, fc2_b):
        import jax, jax.numpy as jnp
        import numpy as np
        EPS = 1e-05

        def layer_norm(x, w, b):
            mu = jnp.mean(x, axis=-1, keepdims=True)
            var = jnp.var(x, axis=-1, keepdims=True)
            return (x - mu) * jax.lax.rsqrt(var + EPS) * w + b
        B, N, C = x.shape
        M = context.shape[1]
        H = 16
        D = C // H
        scale = D ** (-0.5)
        xq = layer_norm(x, qn_w, qn_b)
        ctx = layer_norm(context, cn_w, cn_b)
        q = (xq @ q_w).reshape(B, N, H, D)
        kv = (ctx @ kv_w).reshape(B, M, 2, H, D)
        k, v = (kv[:, :, 0], kv[:, :, 1])
        attn = jnp.einsum('bnhd,bmhd->bhnm', q, k) * scale
        neg = -jnp.finfo(attn.dtype).max
        attn = jnp.where(xa_mask[:, None, :, :], neg, attn)
        attn = jax.nn.softmax(attn, axis=-1)
        out = jnp.einsum('bhnm,bmhd->bnhd', attn, v).reshape(B, N, C)
        out = out @ proj_w + proj_b
        x = x + out
        h = layer_norm(x, n2_w, n2_b)
        h = jax.nn.gelu(h @ fc1_w + fc1_b, approximate=False) @ fc2_w + fc2_b
        return x + h
    x = _L0_xattn_ref(x, ctx_1024, itok_BxS2_4_31999, ctxb_2048x64, L0_xattn_A, L0_xattn_Bmat, L0_xattn_Cmat, L0_xattn_W_in, L0_xattn_b_in, L0_xattn_W_qkv, L0_xattn_b_qkv, L0_xattn_W_o, L0_xattn_b_o, L0_xattn_W_prog, L0_xattn_b_prog, L0_xattn_g1, L0_xattn_beta1, L0_xattn_g2, L0_xattn_beta2)
    x = _L1_xattn_ref(x, ctx_1024, L1_xattn_ln_g, L1_xattn_ln_b, L1_xattn_wq, L1_xattn_bq, L1_xattn_wkv, L1_xattn_bkv, L1_xattn_wo, L1_xattn_bo)
    x = _L2_xattn_ref(x, ctx_1024, ctx_1024, mask_1x1xSxS2_if1, L2_xattn_Wq, L2_xattn_bq, L2_xattn_Wk, L2_xattn_bk, L2_xattn_Wv, L2_xattn_bv, L2_xattn_Wo, L2_xattn_bo, L2_xattn_ln_g, L2_xattn_ln_b)
    x = _L3_xattn_ref(x, ctx_1024, mask_BxSxS2_bk0, L3_xattn_qn_w, L3_xattn_qn_b, L3_xattn_cn_w, L3_xattn_cn_b, L3_xattn_n2_w, L3_xattn_n2_b, L3_xattn_q_w, L3_xattn_kv_w, L3_xattn_proj_w, L3_xattn_proj_b, L3_xattn_fc1_w, L3_xattn_fc1_b, L3_xattn_fc2_w, L3_xattn_fc2_b)
    return x

_drawn_inputs = setup_inputs


def setup_inputs(seed=0):
    import zlib

    import numpy as np

    out = dict(_drawn_inputs(seed))
    spreads = {'L0_xattn_b_in': (0.0, 0.1),
     'L0_xattn_b_qkv': (0.0, 0.1),
     'L0_xattn_b_o': (0.0, 0.1),
     'L0_xattn_b_prog': (0.0, 0.1),
     'L0_xattn_g1': (1.0, 0.2),
     'L0_xattn_beta1': (0.0, 0.1),
     'L0_xattn_g2': (1.0, 0.2),
     'L0_xattn_beta2': (0.0, 0.1),
     'L1_xattn_ln_g': (1.0, 0.6),
     'L1_xattn_ln_b': (0.0, 0.428),
     'L2_xattn_bq': (0.0, 0.605),
     'L2_xattn_bk': (0.0, 2.0),
     'L2_xattn_bv': (0.0, 0.1),
     'L2_xattn_bo': (0.0, 0.1),
     'L2_xattn_ln_g': (1.0, 0.2),
     'L2_xattn_ln_b': (0.0, 0.1),
     'L3_xattn_qn_w': (1.0, 0.2),
     'L3_xattn_qn_b': (0.0, 0.422),
     'L3_xattn_cn_w': (1.0, 0.2),
     'L3_xattn_cn_b': (0.0, 0.1),
     'L3_xattn_n2_w': (1.0, 0.2),
     'L3_xattn_n2_b': (0.0, 0.1),
     'L3_xattn_proj_b': (0.0, 0.1),
     'L3_xattn_fc1_b': (0.0, 0.1),
     'L3_xattn_fc2_b': (0.0, 0.1)}
    factors = {'L1_xattn_wq': 4.419, 'L1_xattn_bq': 30.35, 'L1_xattn_bkv': 5.206, 'L1_xattn_bo': 5.936}
    for name, (base, spread) in spreads.items():
        noise = np.random.default_rng([zlib.crc32(name.encode()), seed]).standard_normal(out[name].shape)
        drawn = base * np.exp(spread * noise) if base else spread * noise
        out[name] = jnp.asarray(drawn.astype(out[name].dtype))
    for name, factor in factors.items():
        out[name] = (out[name] * factor).astype(out[name].dtype)
    return out
```

```python
import concourse.bass as bass
from concourse import mybir
from contextlib import ExitStack

F32 = mybir.dt.float32
BF16 = mybir.dt.bfloat16
I32 = mybir.dt.int32
U8 = mybir.dt.uint8
ALU = mybir.AluOpType
ACT = mybir.ActivationFunctionType
AX = mybir.AxisListType

P = 128
H = 256
KC = H // P
KEYS = 77
HG = 8
HB = 4
GROWS = HG * KEYS
TILES = -(-GROWS // P)
TROWS = [min(P, GROWS - j * P) for j in range(TILES)]
TFIRST = [j * P // KEYS for j in range(TILES)]
TLAST = [(j * P + TROWS[j] - 1) // KEYS for j in range(TILES)]
TSLOT = [sum(TLAST[i] - TFIRST[i] + 1 for i in range(j)) for j in range(TILES + 1)]
PAIR = 2
LANES = 4
NEG = -float(2 ** 100)
EPS = 1e-5
CH = 16
ST = 64


class Attn:

    def __init__(self, name, heads, hd):
        self.name, self.heads, self.hd = name, heads, hd
        self.width = heads * hd
        self.chunks = self.width // P
        self.hpc = P // hd
        self.groups = heads // HG
        self.scale = float(hd) ** -0.5


L0, L1, L2, L3 = Attn("0", 8, 32), Attn("1", 16, 64), Attn("2", 16, 16), Attn("3", 16, 16)
ATTN = {a.name: a for a in (L0, L1, L2, L3)}


def norm_steps(key):
    return [("stats", key), ("aggr", key), ("vareps", key), ("rstd", key), ("norm", key)]


def attention_steps(a):
    steps = [("query", a.name), ("query_add" if a is L1 else "query_bias", a.name)]
    for g in range(a.groups):
        k = f"{a.name}.{g}"
        steps += [("scores", k), ("rowmax", k)]
        if a is L2:
            steps += [("clamp", k)]
        steps += [("shift", k), ("expo", k)]
        if a is L2:
            steps += [("maskmul", k)]
        if a is L1:
            steps += [("rowsum", k), ("recip", k), ("weigh", k)]
        steps += [("pturn", k), ("pturn_main", k), ("pturn_rest", k), ("mix", k)]
        if a is L1:
            steps += [("resid", k)]
        else:
            if a is L2:
                steps += [("den_eps", k)]
            steps += [("recip", k), ("heads", k)]
    if a is not L1:
        o = a.name + "o"
        steps += [("turn", o), ("turned", o), ("proj", a.name), ("resid", a.name)]
    return steps


BEFORE = (norm_steps("0") + [("prebias", "0"), ("turn", "0"), ("turned", "0")] + attention_steps(L0)
          + norm_steps("u") + [("keep", "u"), ("turn", "u"), ("turned", "u"), ("uproj", "u"), ("u_sb", "u")])
AFTER = ([("state", "s"), ("ssm", "s"), ("resume", "s")]
         + norm_steps("1") + [("prebias", "1"), ("turn", "1"), ("turned", "1")] + attention_steps(L1)
         + [("turn", "2"), ("turned", "2"), ("prebias", "2")] + attention_steps(L2)
         + norm_steps("2") + [("gain", "2"), ("offset", "2")]
         + norm_steps("3") + [("prebias", "3"), ("turn", "3"), ("turned", "3")] + attention_steps(L3)
         + norm_steps("m") + [("prebias", "m"), ("turn", "m"), ("turned", "m"),
                              ("fc1", "m"), ("gelu", "m"), ("fc2", "m"), ("resid", "m"), ("store", "m")])


MADE_BY = {
    "tensor": ("turn", "query", "scores", "pturn", "mix", "proj", "uproj", "ssm", "fc1", "fc2"),
    "scalar": ("turned", "query_bias", "expo", "pturn_main", "u_sb", "gelu"),
    "vector": ("stats", "aggr", "norm", "query_add", "rowmax", "clamp", "shift", "rowsum", "den_eps", "recip", "weigh",
               "pturn_rest", "heads", "resid", "resume"),
    "gpsimd": ("vareps", "rstd", "prebias", "keep", "state", "maskmul", "gain", "offset"),
    "sync": ("store",)}
TURNS = [
    {"tensor": "130120120213103120130202323131002323",
     "vector": "113300122302110012211033200113122100330222033323",
     "scalar": "1012021310320123032311023023",
     "gpsimd": "113030221201131002203323"},
    {"tensor": (
        "031020210121302303201212031030201302123121201030323123120130323020212313113030012012013203123102"
        "13231030202321323103102132303121"),
     "vector": (
        "000031312122132003000102101221223112032301032030013202311220211132313033023012032120001130002222"
        "133131122201300313310233322200012023211103032301112123331100123033030112200213113022113233200332"
        "1220300133102223132311132301"),
     "scalar": "012031202310023100213201231021323013023210321313000120123123102331021023323102031231",
     "gpsimd": "03100212120233132001213032130000220022111121132323333000301222113331",
     "sync": "0123"},
]


def in_turn(plan, engine, lanes):
    own = [(s, k) for s, k in plan if s in MADE_BY[engine]]
    at, out = [0] * LANES, []
    for lane in map(int, lanes):
        out.append((*own[at[lane]], lane))
        at[lane] += 1
    assert at == [len(own)] * LANES
    return out


FREED = {"tensor": (("turn", 0), ("scores", 1), ("ssm", 1)), "scalar": (("u_sb", 0),), "vector": (("resid", 1),)}


class Counts:

    def __init__(self, iters):
        self.iters = iters
        self.order = [{e: in_turn(plan, e, TURNS[ph].get(e, "")) for e in MADE_BY}
                      for ph, plan in enumerate((BEFORE, AFTER))]
        self.per = [{}, {}]
        self.index = [{}, {}]
        for ph, order in enumerate(self.order):
            for s, k, lane in (step for steps in order.values() for step in steps):
                self.index[ph][s, k, lane] = self.per[ph].get(s, 0)
                self.per[ph][s] = self.per[ph].get(s, 0) + 1
        self.steps = sorted((set(self.per[0]) | set(self.per[1])) - {"store"})
        self.start = {s: self.per[ph][s] for steps in FREED.values() for s, ph in steps}

    def before_loop(self, ph, pair, step):
        a, b = (self.iters * self.per[q].get(step, 0) for q in (0, 1))
        return pair * (a + b) + (a if ph else 0) + self.start.get(step, 0)

    def tick(self, ph, pair, i):
        return Tick(self, ph, pair, i)


class Tick:

    def __init__(self, counts, ph, pair, i):
        self.c, self.ph, self.pair, self.i = counts, ph, pair, i

    def done(self, step, key, lane):
        c, ph = self.c, self.ph
        return c.before_loop(ph, self.pair, step) + self.i * c.per[ph][step] + c.index[ph][step, key, lane] + 1

    def earlier(self, step, key, lane):
        return self.done(step, key, lane) - self.c.per[self.ph][step]


def xattn_chain(nc, A):
    out = A["out"]
    B, S, _ = A["x"].shape
    NT = S // P
    TPL = LANES // PAIR
    ITERS = NT // TPL
    NCH = S // CH
    PAIRS = B // PAIR
    HID = A["L3_xattn_fc1_w"].shape[1]
    NH = HID // P
    PK = PAIR * KEYS
    counts = Counts(ITERS)

    with ExitStack() as ctx:
        def sb(name, shape, dt=F32):
            return ctx.enter_context(nc.sbuf_tensor(name, shape, dt))

        sems = {}

        def sem(name):
            sems[name] = ctx.enter_context(nc.semaphore(name))
            return sems[name]

        wT = {"0": sb("wT0", [P, KC, 4 * H]), "2": sb("wT2", [P, KC, 4 * H])}
        wq1 = sb("wq1", [P, KC, L1.width])
        wq3 = sb("wq3", [P, KC, H])
        wp3 = sb("wp3", [P, KC, H])
        fc1 = sb("fc1", [P, KC, HID])
        fc2 = sb("fc2", [P, NH, H])
        wU = sb("wU", [P, KC, ST])
        cmat = sb("cmat", [ST, H])
        aT = sb("aT", [ST, ST])
        wprogT = sb("wprogT", [ST, H])
        def cols(name, n):
            return sb(name, [P, n])
        g0, be0, gu, beu = cols("g0", KC), cols("be0", KC), cols("gu", KC), cols("beu", KC)
        g1, be1, g3, be3 = cols("g1", KC), cols("be1", KC), cols("g3", KC), cols("be3", KC)
        gc, bec, gm, bem = cols("gc", KC), cols("bec", KC), cols("gm", KC), cols("bem", KC)
        bqk0, bq1, bkv1 = cols("bqk0", 2 * KC), cols("bq1", L1.chunks), cols("bkv1", 2 * L1.chunks)
        bq2, bk2, bfc1, bin_ = cols("bq2", KC), cols("bk2", KC), cols("bfc1", NH), cols("bin_", KC)
        bU = sb("bU", [ST, 1])
        row_names = ["bo0", "bo1", "bo2", "g2", "be2", "bp3", "bfc2", "bv0", "bv2", "bprog"]
        rows = {n: sb("row_" + n, [P, H]) for n in row_names}
        modrow = sb("modrow", [P, PAIR, H])
        kblk = {a.name: sb("kblk" + a.name, [P, PAIR, a.chunks, a.hpc, KEYS]) for a in ATTN.values()}
        vtab = {a.name: sb("vtab" + a.name, [P, PAIR, a.groups, TSLOT[-1], a.hd + 1]) for a in (L0, L2, L3)}
        vwo = sb("vwo", [P, PAIR, L1.groups, TILES, H])
        neg3 = sb("neg3", [P, PAIR, NT, KEYS], BF16)
        neg2 = sb("neg2", [P, NT, KEYS], BF16)
        mul2 = sb("mul2", [P, NT, KEYS])
        causal = sb("causal", [P, NT, KEYS], BF16)
        ident = sb("ident", [P, P])
        identb = sb("identb", [P, P], BF16)
        hmask = {a.hd: sb(f"hmask{a.hd}", [P, a.hpc]) for a in (L0, L1, L2)}
        tmask = sb("tmask", [P, TILES, HG])
        ones1 = sb("ones1", [1, P])
        mean77 = sb("mean77", [P, 1])
        halfneg = sb("halfneg", [P, 1])
        scan = sb("scan", [P, 2, PAIR * (S + 1)])
        U = scan[0:ST, 0, :].rearrange("p (b t) -> p b t", b=PAIR)
        R = scan[0:ST, 1, :].rearrange("p (b t) -> p b t", b=PAIR)
        NC1 = L1.chunks
        CROWS = L1.hpc * KEYS
        GC = NC1 // L1.groups
        WIDE = 2 * P
        FROM = [(c * CROWS // P) * P - c * CROWS for c in range(GC)]
        vtw = scan[:, :, :].rearrange("p a n -> p (a n)")[:, 0:PAIR * NC1 * WIDE].rearrange(
            "p (b c n) -> p b c n", b=PAIR, c=NC1)
        ends = sb("ends", [ST, PAIR, NCH])
        gap = sb("gap", [ST, 2])
        gmx = sb("gmx", [1, 3])
        agree = sb("agree", [1, 1], I32)
        xs = sb("xs", [P, PAIR, NT, H])
        x = sb("xt", [P, LANES, H])
        z = sb("zt", [P, LANES, H])
        t = sb("tt", [P, LANES, KC, P])
        big = sb("big", [P, LANES, HID])
        pr = sb("pr", [P, LANES, 5 * P])
        stat = sb("stat", [P, LANES, 6])
        mv = sb("mv", [P, LANES, 2])
        rstd = sb("rstd", [P, LANES])
        mx = sb("mx", [P, LANES, HG])
        rec = sb("rec", [P, LANES, HG])
        wkv1 = big[:, :, :].rearrange("p l n -> p (l n)").rearrange("p (k n) -> p k n", k=KC)
        wo1 = pr[:, :, :].rearrange("p l n -> p (l n)")[:, 0:NC1 * H].rearrange("p (c n) -> p c n", c=NC1)
        wkv3 = z[:, :, :].rearrange("p l n -> p (l n)").rearrange("p (k n) -> p k n", k=KC)
        cz = x[0:KEYS, 0:PAIR, :]
        cx = x[0:KEYS, PAIR:2 * PAIR, :]
        ct1 = t[:, :, :, :].rearrange("p l c n -> p (l c n)")[:, 0:KC * PK].rearrange("p (c n) -> p c n", c=KC)
        xflat = xs[:, :, :, :].rearrange("p b t n -> p (b t n)")
        ct3 = {n: xflat[:, k * KC * 3 * PK:(k + 1) * KC * 3 * PK].rearrange("p (c b r n) -> p c b r n", c=KC, b=PAIR, r=3)
               for k, n in enumerate("023")}
        cstat = sb("cstat", [KEYS, PAIR, 6])
        cmv = sb("cmv", [KEYS, PAIR, 2])
        crs = sb("crs", [KEYS, PAIR])
        ktmp = sb("ktmp", [P, 2, PK])
        kflat = ktmp[:, :, :].rearrange("p a b -> p (a b)")
        m3raw = kflat.bitcast(U8)[:, 0:PAIR * NT * KEYS].rearrange("p (b t k) -> p b t k", b=PAIR, t=NT)
        cb = sb("cb", [KEYS, PAIR, ST])
        mT = sb("mT", [ST, PAIR])
        stage = xs[:, :, :, :].rearrange("p b t n -> p (b t) n")
        win = big[:, 0, 0:KC * H].rearrange("p (c n) -> p c n", c=KC)
        bmat = big[:, 1, 0:KC * ST].rearrange("p (c n) -> p c n", c=KC)
        wprog = big[:, 1, 256:256 + KC * ST].rearrange("p (c n) -> p c n", c=KC)
        araw = big[0:ST, 1, 512:512 + ST]
        m2i = z[:, :, :].rearrange("p l n -> p (l n)")[:, 0:NT * KEYS].bitcast(I32).rearrange(
            "p (t k) -> p t k", t=NT)

        ps = ctx.enter_context(nc.psum_tensor("ps", [P, 8, 512], F32))

        done = {s: sem(s + "_done") for s in counts.steps}
        stored = [sem(f"stored{lane}") for lane in range(LANES)]
        stage_in = sem("stage_in")
        weights_in = sem("weights_in")
        consts = sem("consts")
        masks2 = sem("masks2")
        setup_mm, setup_ev = sem("setup_mm"), sem("setup_ev")
        ctx_in = sem("ctx_in")
        tabw_in = sem("tabw_in")
        x_in = sem("x_in")
        ctx_norm = sem("ctx_norm")
        ctx_rstd = sem("ctx_rstd")
        ctx_z = sem("ctx_z")
        tab_mm, tab_act, tab_dve = sem("tab_mm"), sem("tab_act"), sem("tab_dve")
        tab_exp = sem("tab_exp")
        vt_zero, neg3_set = sem("vt_zero"), sem("neg3_set")
        scan_zero, scan_mm, scan_r = sem("scan_zero"), sem("scan_mm"), sem("scan_r")
        ends_kept, gap_set, gap_mm, gap_row, agreed = (
            sem("ends_kept"), sem("gap_set"), sem("gap_mm"), sem("gap_row"), sem("agreed"))
        more_mm, more_r = sem("more_mm"), sem("more_r")
        states_set = sem("states_set")
        passed = {e: sem("passed_" + e) for e in ("pe", "act", "dve", "pool")}
        const_step = sem("const_step")

        ROWBLOCKS = [(n, ("0" if n < 8 else "2"), n % 8) for n in range(16)]
        NSETUP = len(ROWBLOCKS) + 3

        def k_weights(a, kc, c):
            if a is L1:
                return wkv1[:, kc, c * P:(c + 1) * P]
            if a is L3:
                return wkv3[:, kc, c * P:(c + 1) * P]
            return wT[a.name][:, kc, H + c * P:H + (c + 1) * P]

        def v_weights(a, kc):
            if a is L3:
                return wkv3[:, kc, H:2 * H]
            return wT[a.name][:, kc, 2 * H:3 * H]

        def k_ctx(a, kc):
            return ct1[:, kc, :] if a is L1 else ct3[a.name][:, kc, :, 0, :]

        k_bias = {"0": lambda c: bqk0[:, KC + c:KC + c + 1], "1": lambda c: bkv1[:, c:c + 1],
                  "2": lambda c: bk2[:, c:c + 1]}
        ITEMS = [("turnz",), ("turnraw",)]
        ITEMS += [("k", a, c) for a in (L0, L2, L3, L1) for c in range(a.chunks)]
        ITEMS += [("mean",), ("mod", 0), ("mod", 1)]
        ITEMS += [("v", a, b, j) for a in (L0, L2, L3) for b in range(PAIR) for j in range(TILES)]
        ITEMS += [("vt", c) for c in range(NC1)]
        ITEMS += [("vwo", b, g, j) for b in range(PAIR) for g in range(L1.groups) for j in range(TILES)]
        ON_DVE = {"mod", "v", "vwo"}
        act_no, dve_no, k_no = {}, {}, {}
        for n, it in enumerate(ITEMS):
            (dve_no if it[0] in ON_DVE else act_no)[it] = len(dve_no if it[0] in ON_DVE else act_no)
            if it[0] == "k":
                k_no[it] = len(k_no)
        V_DONE = max(dve_no[it] for it in dve_no if it[0] == "v") + 1
        NACT, NDVE, NK, NI = len(act_no), len(dve_no), len(k_no), len(ITEMS)
        BANKS = 8

        def bank(lane, k):
            return ps[:, 2 * lane + k, :]

        def banks(lane):
            return ps[:, 2 * lane:2 * lane + 2, :]

        def stores(pair, i):
            return (pair * ITERS + i) * 16 + 1

        def tile_of(lane, tick):
            return lane % PAIR, tick.i * TPL + lane // PAIR

        def chunk_view(ap2):
            return ap2.rearrange("p b (c l) -> p b c l", l=CH)

        block = ctx.enter_context(nc.Block())

        col_loads = [(g0, "L0_xattn_g1"), (be0, "L0_xattn_beta1"), (gu, "L0_xattn_g2"), (beu, "L0_xattn_beta2"),
                     (g1, "L1_xattn_ln_g"), (be1, "L1_xattn_ln_b"), (g3, "L3_xattn_qn_w"), (be3, "L3_xattn_qn_b"),
                     (gc, "L3_xattn_cn_w"), (bec, "L3_xattn_cn_b"), (gm, "L3_xattn_n2_w"), (bem, "L3_xattn_n2_b"),
                     (bq1, "L1_xattn_bq"), (bkv1, "L1_xattn_bkv"), (bq2, "L2_xattn_bq"), (bk2, "L2_xattn_bk"),
                     (bfc1, "L3_xattn_fc1_b"), (bin_, "L0_xattn_b_in")]
        row_loads = [("bo0", A["L0_xattn_b_o"]), ("bo1", A["L1_xattn_bo"]), ("bo2", A["L2_xattn_bo"]),
                     ("g2", A["L2_xattn_ln_g"]), ("be2", A["L2_xattn_ln_b"]), ("bp3", A["L3_xattn_proj_b"]),
                     ("bfc2", A["L3_xattn_fc2_b"]), ("bv0", A["L0_xattn_b_qkv"][2 * H:3 * H]),
                     ("bv2", A["L2_xattn_bv"]), ("bprog", A["L0_xattn_b_prog"])]
        by_chunk = [(wq1, "L1_xattn_wq"), (wq3, "L3_xattn_q_w"), (wp3, "L3_xattn_proj_w"), (fc1, "L3_xattn_fc1_w"),
                    (fc2, "L3_xattn_fc2_w")]
        NSTAGE = 6 + 5
        NWEIGHTS = len(by_chunk) + 1 + len(col_loads) + 1 + len(row_loads)
        NCTX = 2 + PAIR

        @block.sync
        def _(sp):
            for lane in range(LANES):
                sp.sem_inc(stored[lane], 1)
            sp.dma_start(stage[:, 0:6, :], A["L0_xattn_W_qkv"].rearrange("(c p) n -> p c n", p=P)).then_inc(stage_in, 16)
            sp.dma_start(stage[:, 6:8, :], A["L0_xattn_W_o"].rearrange("(c p) n -> p c n", p=P)).then_inc(stage_in, 16)
            for n, name in enumerate(("Wq", "Wk", "Wv", "Wo")):
                sp.dma_start(stage[:, 8 + 2 * n:10 + 2 * n, :],
                             A["L2_xattn_" + name].rearrange("(c p) n -> p c n", p=P)).then_inc(stage_in, 16)
            sp.dma_start(win, A["L0_xattn_W_in"].rearrange("(c p) n -> p c n", p=P)).then_inc(stage_in, 16)
            sp.dma_start(bmat, A["L0_xattn_Bmat"].rearrange("(c p) n -> p c n", p=P)).then_inc(stage_in, 16)
            sp.dma_start(wprog, A["L0_xattn_W_prog"].rearrange("(c p) n -> p c n", p=P)).then_inc(stage_in, 16)
            sp.dma_start(araw, A["L0_xattn_A"]).then_inc(stage_in, 16)
            sp.dma_start(m2i, A["mask_1x1xSxS2_if1"][0, 0].rearrange("(t p) k -> p t k", p=P)).then_inc(stage_in, 16)
            for dst, name in by_chunk:
                sp.dma_start(dst[:, :, :], A[name].rearrange("(c p) n -> p c n", p=P)).then_inc(weights_in, 16)
            sp.dma_start(cmat[:, :], A["L0_xattn_Cmat"]).then_inc(weights_in, 16)

            with sp.Fori(0, PAIRS) as pair:
                last = counts.before_loop(0, pair, "resid")
                sp.wait_ge(done["resid"], last)
                for lane in range(LANES):
                    sp.wait_ge(stored[lane], stores(pair, 0))
                sp.dma_start(cx[:, :, :], A["ctx_1024"][bass.ds(pair * PAIR, PAIR)].rearrange("b k n -> k b n")).then_inc(ctx_in, 16)
                sp.dma_start(cb[:, :, :], A["ctxb_2048x64"][bass.ds(pair * PAIR, PAIR)].rearrange("b k n -> k b n")).then_inc(ctx_in, 16)
                for b in range(PAIR):
                    sp.dma_start(m3raw[:, b, :, :], A["mask_BxSxS2_bk0"][bass.ds(pair * PAIR + b, 1)].rearrange(
                        "o (t p) k -> p (o t) k", p=P)).then_inc(ctx_in, 16)
                sp.wait_ge(setup_ev, NSETUP)
                sp.wait_ge(masks2, 2)
                sp.dma_start(wkv1, A["L1_xattn_wkv"].rearrange("(c p) n -> p c n", p=P)).then_inc(tabw_in, 16)
                sp.dma_start(wo1, A["L1_xattn_wo"].rearrange("(c p) n -> p c n", p=P)).then_inc(tabw_in, 16)
                sp.dma_start(wkv3, A["L3_xattn_kv_w"].rearrange("(c p) n -> p c n", p=P)).then_inc(tabw_in, 16)
                sp.wait_ge(tab_dve, pair * NDVE + V_DONE)
                for b in range(PAIR):
                    sp.dma_start(xs[:, b, :, :], A["x"][bass.ds(pair * PAIR + b, 1)].rearrange(
                        "o (t p) n -> p (o t) n", p=P)).then_inc(x_in, 16)
                with sp.Fori(0, ITERS) as i:
                    tick = counts.tick(1, pair, i)
                    for _, _, lane in counts.order[1]["sync"]:
                        b, tile = tile_of(lane, tick)
                        sp.wait_ge(done["resid"], tick.done("resid", "m", lane))
                        sp.dma_start(out[bass.ds(pair * PAIR + b, 1), bass.ds(tile * P, P), :].rearrange("o p n -> (o p) n"),
                                     x[:, lane, :]).then_inc(stored[lane], 16)
            for lane in range(LANES):
                sp.wait_ge(stored[lane], stores(PAIRS, 0))

        @block.tensor
        def _(pe):
            mm = nc.tensor.matmul

            for s, _ in FREED["tensor"]:
                pe.sem_inc(done[s], counts.start[s])
            pe.wait_ge(stage_in, NSTAGE * 16)
            pe.wait_ge(consts, 1)
            for n, (src, _, _) in enumerate(ROWBLOCKS):
                if n >= BANKS:
                    pe.wait_ge(setup_ev, n - BANKS + 1)
                for kc in range(KC):
                    last = nc.tensor.transpose(ps[:, n % BANKS, kc * P:(kc + 1) * P], stage[:, src, kc * P:(kc + 1) * P], ident[:, :])
                last.then_inc(setup_mm, 1)
            n = len(ROWBLOCKS)
            pe.wait_ge(setup_ev, n - BANKS + 1)
            for c in range(KC):
                last = nc.tensor.transpose(ps[0:ST, n % BANKS, c * P:(c + 1) * P], wprog[:, c, :], ident[:, :])
            last.then_inc(setup_mm, 1)
            n += 1
            pe.wait_ge(setup_ev, n - BANKS + 1)
            nc.tensor.transpose(ps[0:ST, n % BANKS, 0:ST], araw, ident[0:ST, 0:ST]).then_inc(setup_mm, 1)
            n += 1
            pe.wait_ge(setup_ev, n - BANKS + 1)
            pe.wait_ge(weights_in, NWEIGHTS * 16)
            for kc in range(KC):
                for oc in range(KC):
                    mm(ps[:, n % BANKS, kc * ST:(kc + 1) * ST], win[:, oc, kc * P:(kc + 1) * P], bmat[:, oc, :],
                       start=oc == 0, stop=oc == KC - 1)
            for oc in range(KC):
                last = mm(ps[0:ST, n % BANKS, KC * ST:KC * ST + 1], bmat[:, oc, :], bin_[:, oc:oc + 1],
                          start=oc == 0, stop=oc == KC - 1)
            last.then_inc(setup_mm, 1)

            def tables(pair):
                pe.wait_ge(setup_ev, NSETUP)
                pe.wait_ge(done["resid"], counts.before_loop(0, pair, "resid"))
                for n, it in enumerate(ITEMS):
                    if n >= BANKS:
                        old = ITEMS[n - BANKS]
                        if old[0] in ON_DVE:
                            pe.wait_ge(tab_dve, pair * NDVE + dve_no[old] + 1)
                        else:
                            pe.wait_ge(tab_act, pair * NACT + act_no[old] + 1)
                    bk = ps[:, n % BANKS, :]
                    kind = it[0]
                    if kind == "turnz":
                        pe.wait_ge(ctx_z, pair + 1)
                        for c in range(KC):
                            for b in range(PAIR):
                                o = c * PK + b * KEYS
                                last = nc.tensor.transpose(bk[:, o:o + KEYS], cz[:, b, c * P:(c + 1) * P], ident[0:KEYS, 0:KEYS])
                    elif kind == "turnraw":
                        for c in range(KC):
                            for b in range(PAIR):
                                o = c * PK + b * KEYS
                                last = nc.tensor.transpose(bk[:, o:o + KEYS], cx[:, b, c * P:(c + 1) * P], ident[0:KEYS, 0:KEYS])
                    elif kind == "k":
                        a, c = it[1:]
                        if c == 0:
                            pe.wait_ge(tab_act, pair * NACT + 2)
                            pe.wait_ge(tabw_in, (pair + 1) * 3 * 16)
                        for kc in range(KC):
                            last = mm(bk[:, 0:PK], k_weights(a, kc, c), k_ctx(a, kc), start=kc == 0, stop=kc == KC - 1)
                    elif kind == "mean":
                        for b in range(PAIR):
                            last = mm(bk[0:ST, b:b + 1], cb[:, b, :], mean77[0:KEYS, :], start=True, stop=True)
                    elif kind == "mod":
                        b = it[1]
                        pe.wait_ge(tab_act, pair * NACT + act_no[("mean",)] + 1)
                        last = mm(bk[:, 0:H], mT[:, b:b + 1].to_broadcast([ST, P]), wprogT[:, :], start=True, stop=True)
                    elif kind == "v":
                        a, b, j = it[1:]
                        o, k0 = bk[0:TROWS[j], 0:H], j * P % KEYS
                        for kc in range(KC):
                            keys = ct3[a.name][:, kc, b, :, :].rearrange("p r n -> p (r n)")[:, k0:k0 + TROWS[j]]
                            last = mm(o, keys, v_weights(a, kc), start=kc == 0, stop=a is L3 and kc == KC - 1)
                        if a is not L3:
                            last = mm(o, ones1[:, 0:TROWS[j]], rows["bv" + a.name][0:1, :], start=False, stop=True)
                    elif kind == "vt":
                        c = it[1]
                        for kc in range(KC):
                            last = mm(bk[:, 0:PK], wkv1[:, kc, L1.width + c * P:L1.width + (c + 1) * P], ct1[:, kc, :],
                                      start=kc == 0, stop=kc == KC - 1)
                    else:
                        b, g, j = it[1:]
                        pe.wait_ge(tab_act, (pair + 1) * NACT)
                        c0, c1 = j * P // CROWS, (j * P + TROWS[j] - 1) // CROWS
                        for c in range(c0, c1 + 1):
                            at = j * P - c * CROWS - FROM[c]
                            last = mm(bk[0:TROWS[j], 0:H], vtw[:, b, g * GC + c, at:at + TROWS[j]], wo1[:, g * GC + c, :],
                                      start=c == c0, stop=c == c1)
                    last.then_inc(tab_mm, 1)

            def turn(key, lane, tick):
                if key == "0":
                    pe.wait_ge(done["u_sb"], tick.earlier("u_sb", "u", lane))
                if key in ("0", "u", "1", "3", "m"):
                    pe.wait_ge(done["norm"], tick.done("norm", key, lane))
                    src = z
                elif key == "2":
                    pe.wait_ge(done["resid"], tick.done("resid", "1.1", lane))
                    src = x
                else:
                    pe.wait_ge(done["heads"], tick.done("heads", f"{key[0]}.{ATTN[key[0]].groups - 1}", lane))
                    src = z
                for c in range(KC):
                    last = nc.tensor.transpose(bank(lane, 0)[:, c * P:(c + 1) * P], src[:, lane, c * P:(c + 1) * P], ident[:, :])
                last.then_inc(done["turn"], 1)

            def query(key, lane, tick):
                a = ATTN[key]
                pe.wait_ge(done["turned"], tick.done("turned", key, lane))
                w = {"0": wT["0"], "1": wq1, "2": wT["2"], "3": wq3}[key]
                for c in range(a.chunks):
                    for kc in range(KC):
                        last = mm(bank(lane, c // 4)[:, c % 4 * P:(c % 4 + 1) * P], w[:, kc, c * P:(c + 1) * P], t[:, lane, kc, :],
                                  start=kc == 0, stop=kc == KC - 1)
                last.then_inc(done["query"], 1)

            def scores(key, lane, tick):
                a, g = ATTN[key[0]], int(key[2])
                b, tile = tile_of(lane, tick)
                if g == 0:
                    q = "query_add" if a is L1 else "query_bias"
                    pe.wait_ge(done[q], tick.done(q, a.name, lane))
                elif a is L1:
                    pe.wait_ge(done["resid"], tick.done("resid", "1.0", lane))
                else:
                    pe.wait_ge(done["heads"], tick.done("heads", f"{a.name}.0", lane))
                per_bank = max(1, HB // a.hpc)
                for k in range(2):
                    o = bank(lane, k)
                    if a.hpc <= HB:
                        for n in range(per_bank):
                            c = (g * 2 + k) * per_bank + n
                            last = mm(o[:, n * a.hpc * KEYS:(n + 1) * a.hpc * KEYS], big[:, lane, c * P:(c + 1) * P],
                                      kblk[a.name][:, b, c, :, :], start=n == 0, stop=a is L0, skip_group_check=True)
                    else:
                        last = mm(o[:, 0:HB * KEYS], big[:, lane, g * P:(g + 1) * P],
                                  kblk[a.name][:, b, g, k * HB:(k + 1) * HB, :], start=True, stop=False, skip_group_check=True)
                    if a is not L0:
                        m = {"1": causal[:, bass.ds(tile, 1), :], "2": neg2[:, bass.ds(tile, 1), :],
                             "3": neg3[:, b, bass.ds(tile, 1), :]}[a.name]
                        last = mm(o[:, 0:HB * KEYS], identb[:, :], m.to_broadcast([P, HB, KEYS]),
                                  start=False, stop=True, skip_group_check=True)
                last.then_inc(done["scores"], 1)

            def pturn(key, lane, tick):
                if key[0] == "1":
                    pe.wait_ge(done["weigh"], tick.done("weigh", key, lane))
                elif key[0] == "2":
                    pe.wait_ge(done["maskmul"], tick.done("maskmul", key, lane))
                else:
                    pe.wait_ge(done["expo"], tick.done("expo", key, lane))
                for j in range(TILES):
                    last = nc.tensor.transpose(bank(lane, j // 4)[0:TROWS[j], j % 4 * P:(j % 4 + 1) * P],
                                               pr[:, lane, j * P:j * P + TROWS[j]], ident[:, :])
                last.then_inc(done["pturn"], 1)

            def mix(key, lane, tick):
                a, g = ATTN[key[0]], int(key[2])
                b, _ = tile_of(lane, tick)
                pe.wait_ge(done["pturn_main"], tick.done("pturn_main", key, lane))
                pe.wait_ge(done["pturn_rest"], tick.done("pturn_rest", key, lane))
                o = bank(lane, 0)
                for j in range(TILES):
                    pt = pr[0:TROWS[j], lane, j * P:(j + 1) * P]
                    if a is L1:
                        last = mm(o[:, 0:H], pt, vwo[0:TROWS[j], b, g, j, :], start=j == 0, stop=j == TILES - 1)
                    else:
                        w = a.hd + 1
                        last = mm(o[:, TFIRST[j] * w:(TLAST[j] + 1) * w], pt,
                                  vtab[a.name][0:TROWS[j], b, g, TSLOT[j]:TSLOT[j + 1], :],
                                  start=j == 0, stop=j == TILES - 1, skip_group_check=True)
                last.then_inc(done["mix"], 1)

            def proj(key, lane, tick):
                pe.wait_ge(done["turned"], tick.done("turned", key + "o", lane))
                for kc in range(KC):
                    w = wp3[:, kc, :] if key == "3" else wT[key][:, kc, 3 * H:4 * H]
                    last = mm(bank(lane, 1)[:, 0:H], t[:, lane, kc, :], w, start=kc == 0, stop=kc == KC - 1)
                last.then_inc(done["proj"], 1)

            def uproj(key, lane, tick):
                pe.wait_ge(done["turned"], tick.done("turned", "u", lane))
                for kc in range(KC):
                    last = mm(bank(lane, 0)[0:ST, 0:P], wU[:, kc, :], t[:, lane, kc, :], start=kc == 0, stop=kc == KC - 1)
                last.then_inc(done["uproj"], 1)

            def ssm(key, lane, tick):
                pe.wait_ge(done["state"], tick.done("state", "s", lane))
                mm(bank(lane, 0)[:, 0:H], big[0:ST, lane, 0:P], cmat[:, :], start=True, stop=True).then_inc(done["ssm"], 1)

            def do_fc1(key, lane, tick):
                pe.wait_ge(done["turned"], tick.done("turned", "m", lane))
                for c in range(NH):
                    for kc in range(KC):
                        last = mm(bank(lane, c // 4)[:, c % 4 * P:(c % 4 + 1) * P], fc1[:, kc, c * P:(c + 1) * P], t[:, lane, kc, :],
                                  start=kc == 0, stop=kc == KC - 1)
                last.then_inc(done["fc1"], 1)

            def do_fc2(key, lane, tick):
                pe.wait_ge(done["gelu"], tick.done("gelu", "m", lane))
                for c in range(NH):
                    last = mm(bank(lane, 0)[:, 0:H], big[:, lane, c * P:(c + 1) * P], fc2[:, c, :], start=c == 0, stop=c == NH - 1)
                last.then_inc(done["fc2"], 1)

            def scan_step(n, l, mm_done, r_done, past):
                uin, rin = chunk_view(U[:, :, 0:S]), chunk_view(R[:, :, 0:S])
                o = ps[0:ST, l % 2, 0:PAIR * NCH]
                mm(o, aT[:, :], uin[:, :, :, l], start=True, stop=False)
                pe.wait_ge(r_done, past + n + 1)
                pe.sem_inc(passed["pe"], 1)
                mm(o, aT[:, :], rin[:, :, :, l], start=False, stop=True).then_inc(mm_done, 1)

            def scan_pair(pair):
                pe.wait_ge(done["u_sb"], counts.before_loop(1, pair, "u_sb"))
                pe.wait_ge(scan_zero, (pair + 1) * 2)
                pe.wait_ge(done["keep"], counts.before_loop(1, pair, "keep"))
                pe.sem_inc(passed["pe"], 1)
                with pe.Fori(0, 2) as sweep:
                    for l in range(CH):
                        scan_step(sweep * CH + l, l, scan_mm, scan_r, pair * 2 * CH)
                pe.wait_ge(gap_set, pair + 1)
                pe.sem_inc(passed["pe"], 1)
                for k in range(2):
                    last = nc.tensor.transpose(ps[0:1, 2, k * ST:(k + 1) * ST], gap[:, k:k + 1], ident[0:ST, 0:ST])
                last.then_inc(gap_mm, 1)
                pe.wait_ge(agreed, pair + 1)
                pe.sem_inc(passed["pe"], 1)
                ok = pe.value_load(agree[0:1, 0:1], min_val=0, max_val=1)
                more = (NCH - 2) * CH
                with pe.If(ok == 0):
                    with pe.Fori(0, NCH - 2) as sweep:
                        for l in range(CH):
                            scan_step(sweep * CH + l, l, more_mm, more_r, pair * more)
                with pe.If(ok == 1):
                    pe.sem_inc(more_mm, more)

            steps = {"turn": turn, "query": query, "scores": scores, "pturn": pturn, "mix": mix, "proj": proj,
                     "uproj": uproj, "ssm": ssm, "fc1": do_fc1, "fc2": do_fc2}
            with pe.Fori(0, PAIRS) as pair:
                tables(pair)
                pe.wait_ge(tab_dve, (pair + 1) * NDVE)
                pe.wait_ge(tab_exp, (pair + 1) * NK)
                pe.wait_ge(neg3_set, pair + 1)
                pe.sem_inc(passed["pe"], 1)
                with pe.Fori(0, ITERS) as i:
                    tick = counts.tick(0, pair, i)
                    for s, key, lane in counts.order[0]["tensor"]:
                        steps[s](key, lane, tick)
                scan_pair(pair)
                with pe.Fori(0, ITERS) as i:
                    tick = counts.tick(1, pair, i)
                    for s, key, lane in counts.order[1]["tensor"]:
                        steps[s](key, lane, tick)

        @block.scalar
        def _(act):
            ac = nc.scalar.activation
            for s, _ in FREED["scalar"]:
                act.sem_inc(done[s], counts.start[s])
            act.sem_inc(scan_r, 1)
            act.sem_inc(more_r, 1)
            for dst, name in col_loads:
                act.dma_start(dst[:, :], A[name].rearrange("(c p) -> p c", p=P), allow_slow_non_contiguous=True).then_inc(weights_in, 16)
            act.dma_start(bqk0[:, :], A["L0_xattn_b_qkv"][0:2 * H].rearrange("(c p) -> p c", p=P),
                          allow_slow_non_contiguous=True).then_inc(weights_in, 16)
            for n, v in row_loads:
                act.dma_start(rows[n][:, :], v.partition_broadcast(P)).then_inc(weights_in, 16)
            act.wait_ge(weights_in, NWEIGHTS * 16)

            def tables(pair):
                for n, it in enumerate(ITEMS):
                    if it[0] in ON_DVE:
                        continue
                    bk = ps[:, n % BANKS, :]
                    act.wait_ge(tab_mm, pair * NI + n + 1)
                    kind = it[0]
                    if kind == "turnz":
                        for c in range(KC):
                            src = bk[:, c * PK:(c + 1) * PK]
                            ac(ct1[:, c, :], src, ACT.Identity, bias=be1[:, c:c + 1], scale=g1[:, c:c + 1])
                            src = src.rearrange("p (b n) -> p b n", b=PAIR).unsqueeze(2).to_broadcast([P, PAIR, 3, KEYS])
                            ac(ct3["0"][:, c], src, ACT.Identity, bias=be0[:, c:c + 1], scale=g0[:, c:c + 1])
                            last = ac(ct3["3"][:, c], src, ACT.Identity, bias=bec[:, c:c + 1], scale=gc[:, c:c + 1])
                    elif kind == "turnraw":
                        for c in range(KC):
                            src = bk[:, c * PK:(c + 1) * PK].rearrange("p (b n) -> p b n", b=PAIR).unsqueeze(2)
                            last = ac(ct3["2"][:, c], src.to_broadcast([P, PAIR, 3, KEYS]), ACT.Copy)
                    elif kind == "k":
                        a, c = it[1:]
                        m = k_no[it]
                        if m == 0:
                            act.wait_ge(neg3_set, pair + 1)
                        if m >= 2:
                            act.wait_ge(tab_exp, pair * NK + m - 1)
                        if a is L3:
                            last = ac(ktmp[:, m % 2, :], bk[:, 0:PK], ACT.Copy)
                        else:
                            last = ac(ktmp[:, m % 2, :], bk[:, 0:PK], ACT.Identity, bias=k_bias[a.name](c))
                        last.then_inc(tab_act, 1)
                        continue
                    elif kind == "mean":
                        last = ac(mT[:, :], bk[0:ST, 0:PAIR], ACT.Copy)
                    else:
                        c = it[1]
                        act.wait_ge(vt_zero, pair + 1)
                        v = bk[:, 0:PK].rearrange("p (b k) -> p b k", b=PAIR)
                        for n2 in range(L1.hpc):
                            h = slice(n2 * L1.hd, (n2 + 1) * L1.hd)
                            at = n2 * KEYS - FROM[c % GC]
                            last = ac(vtw[h, :, c, at:at + KEYS], v[h, :, :], ACT.Identity, bias=bkv1[h, NC1 + c:NC1 + c + 1])
                    last.then_inc(tab_act, 1)

            def turned(key, lane, tick):
                act.wait_ge(done["turn"], tick.done("turn", key, lane))
                affine = {"0": (g0, be0), "u": (gu, beu), "1": (g1, be1), "3": (g3, be3), "m": (gm, bem)}
                if key in affine:
                    gain, bias = affine[key]
                    for c in range(KC):
                        last = ac(t[:, lane, c, :], bank(lane, 0)[:, c * P:(c + 1) * P], ACT.Identity,
                                  bias=bias[:, c:c + 1], scale=gain[:, c:c + 1])
                else:
                    last = ac(t[:, lane, :, :].rearrange("p c n -> p (c n)"), bank(lane, 0)[:, 0:H], ACT.Copy)
                last.then_inc(done["turned"], 1)

            def query_bias(key, lane, tick):
                act.wait_ge(done["query"], tick.done("query", key, lane))
                if key == "3":
                    last = ac(big[:, lane, 0:H], bank(lane, 0)[:, 0:H], ACT.Copy)
                else:
                    bias = bqk0 if key == "0" else bq2
                    for c in range(KC):
                        last = ac(big[:, lane, c * P:(c + 1) * P], bank(lane, 0)[:, c * P:(c + 1) * P], ACT.Identity,
                                  bias=bias[:, c:c + 1])
                last.then_inc(done["query_bias"], 1)

            def expo(key, lane, tick):
                act.wait_ge(done["shift"], tick.done("shift", key, lane))
                v = pr[:, lane, 0:HG * KEYS]
                ac(v, v, ACT.Exp, scale=ATTN[key[0]].scale).then_inc(done["expo"], 1)

            def pturn_main(key, lane, tick):
                act.wait_ge(done["pturn"], tick.done("pturn", key, lane))
                ac(pr[:, lane, 0:4 * P], bank(lane, 0), ACT.Copy).then_inc(done["pturn_main"], 1)

            def u_sb(key, lane, tick):
                b, tile = tile_of(lane, tick)
                act.wait_ge(done["uproj"], tick.done("uproj", "u", lane))
                ac(U[:, b, bass.ds(tile * P + 1, P)], bank(lane, 0)[0:ST, 0:P], ACT.Identity, bias=bU[:, :]).then_inc(done["u_sb"], 1)

            def gelu(key, lane, tick):
                act.wait_ge(done["fc1"], tick.done("fc1", "m", lane))
                for c in range(NH):
                    last = ac(big[:, lane, c * P:(c + 1) * P], bank(lane, c // 4)[:, c % 4 * P:(c % 4 + 1) * P], ACT.Gelu,
                              bias=bfc1[:, c:c + 1])
                last.then_inc(done["gelu"], 1)

            def scan_step(n, l, mm_done, r_done, past):
                rout = chunk_view(R[:, :, 1:S + 1])
                act.wait_ge(mm_done, past + n + 1)
                ac(rout[:, :, :, l], ps[0:ST, l % 2, 0:PAIR * NCH].rearrange("p (b c) -> p b c", b=PAIR),
                   ACT.Silu).then_inc(r_done, 1)

            def scan_pair(pair):
                with act.Fori(0, 2) as sweep:
                    act.wait_ge(ends_kept, pair * 2 + sweep + 1)
                    for l in range(CH):
                        scan_step(sweep * CH + l, l, scan_mm, scan_r, pair * 2 * CH)
                act.wait_ge(agreed, pair + 1)
                act.sem_inc(passed["act"], 1)
                ok = act.value_load(agree[0:1, 0:1], min_val=0, max_val=1)
                more = (NCH - 2) * CH
                with act.If(ok == 0):
                    with act.Fori(0, NCH - 2) as sweep:
                        for l in range(CH):
                            scan_step(sweep * CH + l, l, more_mm, more_r, pair * more)
                with act.If(ok == 1):
                    act.sem_inc(more_r, more)

            steps = {"turned": turned, "query_bias": query_bias, "expo": expo, "pturn_main": pturn_main, "u_sb": u_sb,
                     "gelu": gelu}
            with act.Fori(0, PAIRS) as pair:
                tables(pair)
                act.wait_ge(scan_zero, (pair + 1) * 2)
                with act.Fori(0, ITERS) as i:
                    tick = counts.tick(0, pair, i)
                    for s, key, lane in counts.order[0]["scalar"]:
                        steps[s](key, lane, tick)
                scan_pair(pair)
                with act.Fori(0, ITERS) as i:
                    tick = counts.tick(1, pair, i)
                    for s, key, lane in counts.order[1]["scalar"]:
                        steps[s](key, lane, tick)

        @block.vector
        def _(dve):
            v = nc.vector
            for s, _ in FREED["vector"]:
                dve.sem_inc(done[s], counts.start[s])
            dve.sem_inc(ends_kept, 1)
            for n, (_, layer, blk) in enumerate(ROWBLOCKS):
                dve.wait_ge(setup_mm, n + 1)
                v.tensor_copy(wT[layer][:, :, blk * P:(blk + 1) * P],
                              ps[:, n % BANKS, 0:KC * P].rearrange("p (c n) -> p c n", c=KC)).then_inc(setup_ev, 1)
            n = len(ROWBLOCKS)
            dve.wait_ge(setup_mm, n + 1)
            v.tensor_copy(wprogT[:, :], ps[0:ST, n % BANKS, 0:H]).then_inc(setup_ev, 1)
            n += 1
            dve.wait_ge(setup_mm, n + 1)
            v.tensor_copy(aT[:, :], ps[0:ST, n % BANKS, 0:ST]).then_inc(setup_ev, 1)
            n += 1
            dve.wait_ge(setup_mm, n + 1)
            v.tensor_copy(bU[:, :], ps[0:ST, n % BANKS, KC * ST:KC * ST + 1])
            v.tensor_copy(wU[:, :, :].rearrange("p c n -> p (c n)"), ps[:, n % BANKS, 0:KC * ST]).then_inc(setup_ev, 1)
            dve.wait_ge(weights_in, NWEIGHTS * 16)
            dve.wait_ge(consts, 1)
            for a in (L0, L2, L3):
                for b in range(PAIR):
                    for g in range(a.groups):
                        for j in range(TILES):
                            v.tensor_copy(vtab[a.name][:, b, g, TSLOT[j]:TSLOT[j + 1], a.hd:a.hd + 1],
                                          tmask[:, j, TFIRST[j]:TLAST[j] + 1].unsqueeze(2))

            def tables(pair):
                dve.wait_ge(ctx_in, (pair + 1) * NCTX * 16)
                dve.wait_ge(done["resid"], counts.before_loop(0, pair, "resid"))
                for lane in range(LANES):
                    dve.wait_ge(stored[lane], stores(pair, 0))
                for b in range(PAIR):
                    v.bn_stats(cstat[:, b, :], cx[:, b, :]).then_inc(ctx_norm, 1)
                dve.wait_ge(ctx_norm, pair * 2 * PAIR + PAIR)
                dve.sem_inc(passed["dve"], 1)
                for b in range(PAIR):
                    v.bn_aggr(cmv[:, b, :], cstat[:, b, :]).then_inc(ctx_norm, 1)
                dve.wait_ge(ctx_rstd, pair * 2 + 2)
                for b in range(PAIR):
                    last = v.tensor_scalar(cz[:, b, :], cx[:, b, :], cmv[:, b, 0:1], crs[:, b:b + 1], ALU.subtract, ALU.mult)
                last.then_inc(ctx_z, 1)
                for n, it in enumerate(ITEMS):
                    kind = it[0]
                    bk = ps[:, n % BANKS, :]
                    if kind == "k":
                        a, c = it[1:]
                        m = k_no[it]
                        dve.wait_ge(tab_act, pair * NACT + act_no[it] + 1)
                        for b in range(PAIR):
                            last = v.tensor_tensor(
                                kblk[a.name][:, b, c, :, :],
                                ktmp[:, m % 2, b * KEYS:(b + 1) * KEYS].unsqueeze(1).to_broadcast([P, a.hpc, KEYS]),
                                hmask[a.hd][:, :].unsqueeze(2).to_broadcast([P, a.hpc, KEYS]), ALU.mult)
                        last.then_inc(tab_exp, 1)
                        continue
                    if kind not in ON_DVE:
                        continue
                    dve.wait_ge(tab_mm, pair * NI + n + 1)
                    if kind == "mod":
                        last = v.tensor_tensor(modrow[:, it[1], :], bk[:, 0:H], rows["bprog"][:, :], ALU.add)
                    elif kind == "v":
                        a, b, j = it[1:]
                        src = bk[0:TROWS[j], 0:H].rearrange("p (g h d) -> p g h d", h=HG, d=a.hd)
                        h = slice(TFIRST[j], TLAST[j] + 1)
                        for g in range(a.groups):
                            o = vtab[a.name][0:TROWS[j], b, g, TSLOT[j]:TSLOT[j + 1], 0:a.hd]
                            last = v.tensor_tensor(o, src[:, g, h, :], tmask[0:TROWS[j], j, h].unsqueeze(2).to_broadcast(list(o.shape)),
                                                   ALU.mult)
                    else:
                        b, g, j = it[1:]
                        last = v.tensor_copy(vwo[0:TROWS[j], b, g, j, :], bk[0:TROWS[j], 0:H])
                    last.then_inc(tab_dve, 1)

            def src_of(key, lane, tick):
                if key == "0":
                    b, tile = tile_of(lane, tick)
                    return xs[:, b, bass.ds(tile, 1), :].rearrange("p o n -> p (o n)")
                return x[:, lane, :]

            def stats(key, lane, tick):
                before = {"u": ("resid", "0"), "1": ("resume", "s"), "2": ("resid", "2"), "3": ("offset", "2"), "m": ("resid", "3")}
                if key in before:
                    s, k = before[key]
                    dve.wait_ge(done[s], tick.done(s, k, lane))
                v.bn_stats(stat[:, lane, :], src_of(key, lane, tick)).then_inc(done["stats"], 1)

            def aggr(key, lane, tick):
                dve.wait_ge(done["stats"], tick.done("stats", key, lane))
                dve.sem_inc(passed["dve"], 1)
                v.bn_aggr(mv[:, lane, :], stat[:, lane, :]).then_inc(done["aggr"], 1)

            def norm(key, lane, tick):
                if key == "0":
                    dve.wait_ge(done["turn"], tick.earlier("turn", "u", lane))
                dve.wait_ge(done["rstd"], tick.done("rstd", key, lane))
                v.tensor_scalar(z[:, lane, :], src_of(key, lane, tick), mv[:, lane, 0:1], rstd[:, lane:lane + 1],
                                ALU.subtract, ALU.mult).then_inc(done["norm"], 1)

            def query_add(key, lane, tick):
                dve.wait_ge(done["query"], tick.done("query", key, lane))
                v.tensor_tensor(big[:, lane, :].rearrange("p (c n) -> p c n", n=P),
                                banks(lane).rearrange("p k (c n) -> p (k c) n", n=P),
                                bq1[:, :].unsqueeze(2).to_broadcast([P, L1.chunks, P]), ALU.add).then_inc(done["query_add"], 1)

            def score_view(lane):
                return banks(lane)[:, :, 0:HB * KEYS].rearrange("p k (h n) -> p k h n", n=KEYS)

            def rowmax(key, lane, tick):
                dve.wait_ge(done["scores"], tick.done("scores", key, lane))
                v.tensor_reduce(mx[:, lane, :].rearrange("p (k h) -> p k h", k=2), score_view(lane), AX.X, ALU.max)\
                    .then_inc(done["rowmax"], 1)

            def clamp(key, lane, tick):
                dve.wait_ge(done["rowmax"], tick.done("rowmax", key, lane))
                v.tensor_scalar(mx[:, lane, :], mx[:, lane, :], -1e9 / L2.scale, None, ALU.max).then_inc(done["clamp"], 1)

            def shift(key, lane, tick):
                s = "clamp" if key[0] == "2" else "rowmax"
                dve.wait_ge(done[s], tick.done(s, key, lane))
                v.tensor_tensor(pr[:, lane, 0:HG * KEYS].rearrange("p (k h n) -> p k h n", k=2, n=KEYS), score_view(lane),
                                mx[:, lane, :].rearrange("p (k h) -> p k h", k=2).unsqueeze(3).to_broadcast([P, 2, HB, KEYS]),
                                ALU.subtract).then_inc(done["shift"], 1)

            def rowsum(key, lane, tick):
                dve.wait_ge(done["expo"], tick.done("expo", key, lane))
                v.tensor_reduce(mx[:, lane, :], pr[:, lane, 0:HG * KEYS].rearrange("p (h n) -> p h n", n=KEYS), AX.X, ALU.add)\
                    .then_inc(done["rowsum"], 1)

            def mixed(key, lane):
                a = ATTN[key[0]]
                return bank(lane, 0)[:, 0:HG * (a.hd + 1)].rearrange("p (h d) -> p h d", d=a.hd + 1)

            def den_eps(key, lane, tick):
                dve.wait_ge(done["mix"], tick.done("mix", key, lane))
                v.tensor_scalar(mx[:, lane, :].unsqueeze(2), mixed(key, lane)[:, :, L2.hd:L2.hd + 1], 1e-9, None, ALU.add)\
                    .then_inc(done["den_eps"], 1)

            def recip(key, lane, tick):
                if key[0] == "1":
                    dve.wait_ge(done["rowsum"], tick.done("rowsum", key, lane))
                    src = mx[:, lane, :]
                elif key[0] == "2":
                    dve.wait_ge(done["den_eps"], tick.done("den_eps", key, lane))
                    src = mx[:, lane, :]
                else:
                    dve.wait_ge(done["mix"], tick.done("mix", key, lane))
                    hd = ATTN[key[0]].hd
                    src = mixed(key, lane)[:, :, hd:hd + 1].rearrange("p h o -> p (h o)")
                v.reciprocal(rec[:, lane, :], src).then_inc(done["recip"], 1)

            def weigh(key, lane, tick):
                dve.wait_ge(done["recip"], tick.done("recip", key, lane))
                p8 = pr[:, lane, 0:HG * KEYS].rearrange("p (h n) -> p h n", n=KEYS)
                v.tensor_tensor(p8, p8, rec[:, lane, :].unsqueeze(2).to_broadcast([P, HG, KEYS]), ALU.mult).then_inc(done["weigh"], 1)

            def pturn_rest(key, lane, tick):
                dve.wait_ge(done["pturn"], tick.done("pturn", key, lane))
                v.tensor_copy(pr[0:TROWS[-1], lane, 4 * P:5 * P], bank(lane, 1)[0:TROWS[-1], 0:P]).then_inc(done["pturn_rest"], 1)

            def heads(key, lane, tick):
                a, g = ATTN[key[0]], int(key[2])
                dve.wait_ge(done["recip"], tick.done("recip", key, lane))
                w = HG * a.hd
                v.tensor_tensor(z[:, lane, g * w:(g + 1) * w].rearrange("p (h d) -> p h d", d=a.hd),
                                mixed(key, lane)[:, :, 0:a.hd],
                                rec[:, lane, :].unsqueeze(2).to_broadcast([P, HG, a.hd]), ALU.mult).then_inc(done["heads"], 1)

            def resid(key, lane, tick):
                if key[0] == "1":
                    dve.wait_ge(done["mix"], tick.done("mix", key, lane))
                    src = bank(lane, 0)
                    if key[2] == "0":
                        dve.wait_ge(done["prebias"], tick.done("prebias", "1", lane))
                    else:
                        dve.wait_ge(done["resid"], tick.done("resid", "1.0", lane))
                else:
                    dve.wait_ge(done["prebias"], tick.done("prebias", key, lane))
                    s = "fc2" if key == "m" else "proj"
                    dve.wait_ge(done[s], tick.done(s, key, lane))
                    src = bank(lane, 0 if key == "m" else 1)
                v.tensor_tensor(x[:, lane, :], x[:, lane, :], src[:, 0:H], ALU.add).then_inc(done["resid"], 1)

            def resume(key, lane, tick):
                b, tile = tile_of(lane, tick)
                dve.wait_ge(done["ssm"], tick.done("ssm", "s", lane))
                dve.wait_ge(stored[lane], stores(tick.pair, tick.i))
                v.tensor_tensor(x[:, lane, :], xs[:, b, bass.ds(tile, 1), :].rearrange("p o n -> p (o n)"),
                                bank(lane, 0)[:, 0:H], ALU.add).then_inc(done["resume"], 1)

            def scan_pair(pair):
                ends_now = chunk_view(R[:, :, 1:S + 1])[:, :, :, CH - 1]
                dve.wait_ge(scan_r, pair * 2 * CH + CH + 1)
                v.tensor_copy(ends[:, :, :], ends_now).then_inc(ends_kept, 1)
                dve.wait_ge(scan_r, (pair + 1) * 2 * CH + 1)
                dve.wait_ge(ends_kept, pair * 2 + 2)
                v.tensor_reduce(gap[:, 1:2], ends_now, AX.XY, ALU.max, apply_absolute_value=True)
                v.tensor_tensor(ends[:, :, :], ends[:, :, :], ends_now, ALU.subtract).then_inc(ends_kept, 1)
                dve.wait_ge(ends_kept, pair * 2 + 3)
                v.tensor_reduce(gap[:, 0:1], ends[:, :, :], AX.XY, ALU.max, apply_absolute_value=True).then_inc(gap_set, 1)
                dve.wait_ge(gap_mm, pair + 1)
                v.tensor_reduce(gmx[:, 0:2], ps[0:1, 2, 0:2 * ST].rearrange("p (k n) -> p k n", k=2), AX.X, ALU.max).then_inc(gap_row, 1)
                dve.wait_ge(gap_row, pair * 2 + 1)
                v.tensor_scalar(gmx[:, 2:3], gmx[:, 1:2], 2.0 ** -20, None, ALU.mult).then_inc(gap_row, 1)
                dve.wait_ge(gap_row, pair * 2 + 2)
                v.tensor_tensor(agree[:, :], gmx[:, 0:1], gmx[:, 2:3], ALU.is_le).then_inc(agreed, 1)
                dve.wait_ge(more_r, (pair + 1) * (NCH - 2) * CH + 1)
                v.tensor_tensor(R[:, :, 1:S + 1], R[:, :, 1:S + 1], U[:, :, 1:S + 1], ALU.add).then_inc(states_set, 1)

            steps = {"stats": stats, "aggr": aggr, "norm": norm, "query_add": query_add, "rowmax": rowmax, "clamp": clamp,
                     "shift": shift, "rowsum": rowsum, "den_eps": den_eps, "recip": recip, "weigh": weigh,
                     "pturn_rest": pturn_rest, "heads": heads, "resid": resid, "resume": resume}
            with dve.Fori(0, PAIRS) as pair:
                tables(pair)
                dve.wait_ge(x_in, (pair + 1) * PAIR * 16)
                dve.sem_inc(passed["dve"], 1)
                with dve.Fori(0, ITERS) as i:
                    tick = counts.tick(0, pair, i)
                    for s, key, lane in counts.order[0]["vector"]:
                        steps[s](key, lane, tick)
                scan_pair(pair)
                with dve.Fori(0, ITERS) as i:
                    tick = counts.tick(1, pair, i)
                    for s, key, lane in counts.order[1]["vector"]:
                        steps[s](key, lane, tick)

        @block.gpsimd
        def _(pool):
            p = nc.gpsimd
            n = [0]

            def made(ins):
                ins.then_inc(const_step, 1)
                n[0] += 1
                pool.wait_ge(const_step, n[0])

            made(p.memset(ident[:, :], 0.0))
            made(p.affine_select(out=ident[:, :], in_=ident[:, :], compare_op=ALU.not_equal, fill=1.0, base=0,
                                 pattern=[[-1, P]], channel_multiplier=1))
            made(p.tensor_copy(identb[:, :], ident[:, :]))
            masks = [(hmask[a.hd][:, :], a.hd, a.hpc) for a in (L0, L1, L2)]
            for m, d, h in masks:
                made(p.memset(m, 1.0))
                made(p.affine_select(out=m, in_=m, compare_op=ALU.is_ge, fill=0.0, base=0, pattern=[[-d, h]], channel_multiplier=1))
                made(p.affine_select(out=m, in_=m, compare_op=ALU.is_ge, fill=0.0, base=d - 1, pattern=[[d, h]], channel_multiplier=-1))
            made(p.memset(tmask[:, :, :], 1.0))
            made(p.affine_select(out=tmask[:, :, :], in_=tmask[:, :, :], compare_op=ALU.is_ge, fill=0.0, base=0,
                                 pattern=[[P, TILES], [-KEYS, HG]], channel_multiplier=1))
            made(p.affine_select(out=tmask[:, :, :], in_=tmask[:, :, :], compare_op=ALU.is_ge, fill=0.0, base=KEYS - 1,
                                 pattern=[[-P, TILES], [KEYS, HG]], channel_multiplier=-1))
            made(p.memset(ones1[:, :], 1.0))
            made(p.memset(mean77[:, :], 1.0 / KEYS))
            made(p.memset(halfneg[:, :], -0.5))
            made(p.memset(causal[:, :, :], 0.0))
            p.affine_select(out=causal[:, :, :], in_=causal[:, :, :], compare_op=ALU.is_ge, fill=NEG, base=0,
                            pattern=[[P, NT], [-1, KEYS]], channel_multiplier=1).then_inc(consts, 1)
            pool.wait_ge(stage_in, NSTAGE * 16)
            p.tensor_copy(mul2[:, :, :], m2i).then_inc(masks2, 1)
            pool.wait_ge(masks2, 1)
            p.tensor_scalar(neg2[:, :, :], mul2[:, :, :], 0.0, NEG, ALU.is_equal, ALU.mult).then_inc(masks2, 1)
            pool.wait_ge(weights_in, NWEIGHTS * 16)

            def tables(pair):
                pool.wait_ge(done["ssm"], counts.before_loop(0, pair, "ssm"))
                pool.sem_inc(passed["pool"], 1)
                p.memset(vtw, 0.0).then_inc(vt_zero, 1)
                pool.wait_ge(ctx_in, (pair + 1) * NCTX * 16)
                pool.wait_ge(done["scores"], counts.before_loop(0, pair, "scores"))
                pool.sem_inc(passed["pool"], 1)
                p.tensor_scalar(neg3[:, :, :, :], m3raw[:, :, :, :], NEG, None, ALU.mult).then_inc(neg3_set, 1)
                pool.wait_ge(ctx_norm, (pair + 1) * 2 * PAIR)
                pool.sem_inc(passed["pool"], 1)
                p.tensor_scalar(crs[:, :].unsqueeze(2), cmv[:, :, 1:2], EPS, None, ALU.add).then_inc(ctx_rstd, 1)
                pool.wait_ge(ctx_rstd, pair * 2 + 1)
                pool.sem_inc(passed["pool"], 1)
                p.tensor_tensor(crs[:, :], crs[:, :], halfneg[0:KEYS, :].to_broadcast([KEYS, PAIR]), ALU.pow).then_inc(ctx_rstd, 1)
                pool.wait_ge(tab_dve, (pair + 1) * NDVE)
                pool.sem_inc(passed["pool"], 1)
                p.memset(U[:, :, 0:1], 0.0).then_inc(scan_zero, 1)
                p.memset(chunk_view(R[:, :, 0:S])[:, :, :, 0], 0.0).then_inc(scan_zero, 1)

            def vareps(key, lane, tick):
                pool.wait_ge(done["aggr"], tick.done("aggr", key, lane))
                pool.sem_inc(passed["pool"], 1)
                p.tensor_scalar(rstd[:, lane:lane + 1], mv[:, lane, 1:2], EPS, None, ALU.add).then_inc(done["vareps"], 1)

            def do_rstd(key, lane, tick):
                pool.wait_ge(done["vareps"], tick.done("vareps", key, lane))
                pool.sem_inc(passed["pool"], 1)
                r = rstd[:, lane:lane + 1]
                p.tensor_tensor(r, r, halfneg[:, :], ALU.pow).then_inc(done["rstd"], 1)

            def prebias(key, lane, tick):
                row = rows[{"0": "bo0", "1": "bo1", "2": "bo2", "3": "bp3", "m": "bfc2"}[key]]
                src = x[:, lane, :]
                if key == "2":
                    pool.wait_ge(done["turn"], tick.done("turn", "2", lane))
                else:
                    pool.wait_ge(done["norm"], tick.done("norm", key, lane))
                if key == "0":
                    b, tile = tile_of(lane, tick)
                    src = xs[:, b, bass.ds(tile, 1), :].rearrange("p o n -> p (o n)")
                pool.sem_inc(passed["pool"], 1)
                p.tensor_tensor(x[:, lane, :], src, row[:, :], ALU.add).then_inc(done["prebias"], 1)

            def keep(key, lane, tick):
                b, tile = tile_of(lane, tick)
                pool.wait_ge(done["resid"], tick.done("resid", "0", lane))
                pool.sem_inc(passed["pool"], 1)
                p.tensor_tensor(xs[:, b, bass.ds(tile, 1), :].rearrange("p o n -> p (o n)"), x[:, lane, :], modrow[:, b, :],
                                ALU.add).then_inc(done["keep"], 1)

            def state(key, lane, tick):
                b, tile = tile_of(lane, tick)
                pool.wait_ge(done["resid"], tick.earlier("resid", "m", lane))
                pool.sem_inc(passed["pool"], 1)
                p.tensor_copy(big[0:ST, lane, 0:P], R[:, b, bass.ds(tile * P + 1, P)]).then_inc(done["state"], 1)

            def maskmul(key, lane, tick):
                _, tile = tile_of(lane, tick)
                pool.wait_ge(done["expo"], tick.done("expo", key, lane))
                pool.sem_inc(passed["pool"], 1)
                p8 = pr[:, lane, 0:HG * KEYS].rearrange("p (h n) -> p h n", n=KEYS)
                p.tensor_tensor(p8, p8, mul2[:, bass.ds(tile, 1), :].to_broadcast([P, HG, KEYS]), ALU.mult).then_inc(done["maskmul"], 1)

            def gain(key, lane, tick):
                pool.wait_ge(done["norm"], tick.done("norm", "2", lane))
                pool.sem_inc(passed["pool"], 1)
                p.tensor_tensor(x[:, lane, :], z[:, lane, :], rows["g2"][:, :], ALU.mult).then_inc(done["gain"], 1)

            def offset(key, lane, tick):
                pool.wait_ge(done["gain"], tick.done("gain", "2", lane))
                pool.sem_inc(passed["pool"], 1)
                p.tensor_tensor(x[:, lane, :], x[:, lane, :], rows["be2"][:, :], ALU.add).then_inc(done["offset"], 1)

            steps = {"vareps": vareps, "rstd": do_rstd, "prebias": prebias, "keep": keep, "state": state, "maskmul": maskmul,
                     "gain": gain, "offset": offset}
            with pool.Fori(0, PAIRS) as pair:
                tables(pair)
                pool.wait_ge(x_in, (pair + 1) * PAIR * 16)
                pool.sem_inc(passed["pool"], 1)
                with pool.Fori(0, ITERS) as i:
                    tick = counts.tick(0, pair, i)
                    for s, key, lane in counts.order[0]["gpsimd"]:
                        steps[s](key, lane, tick)
                pool.wait_ge(states_set, pair + 1)
                pool.sem_inc(passed["pool"], 1)
                with pool.Fori(0, ITERS) as i:
                    tick = counts.tick(1, pair, i)
                    for s, key, lane in counts.order[1]["gpsimd"]:
                        steps[s](key, lane, tick)


_UNUSED = ["itok_BxS2_4_31999"]


def kernel(**inputs):
    import numpy as _np
    import concourse.bacc as _bacc
    from concourse import mybir as _mybir
    from concourse.bass_utils import run_bass_kernel_spmd as _run

    nc = _bacc.Bacc("TRN2", target_bir_lowering=False, num_devices=1)
    arrays, args = {}, {}
    for name in inputs:
        if name in _UNUSED:
            continue
        a = _np.ascontiguousarray(inputs[name])
        arrays[f"in_{name}_dram"] = a
        args[name] = nc.dram_tensor(f"in_{name}_dram", a.shape, _mybir.dt.from_np(a.dtype), kind="ExternalInput").ap()
    shape = inputs["x"].shape
    args["out"] = nc.dram_tensor("out_0_dram", shape, _mybir.dt.float32, kind="ExternalOutput").ap()
    xattn_chain(nc, args)
    r = _run(nc, [arrays], core_ids=[0])
    return r.results[0]["out_0_dram"]
```

```python
import concourse.bass as bass
from concourse import mybir
from contextlib import ExitStack

F32 = mybir.dt.float32
BF16 = mybir.dt.bfloat16
I32 = mybir.dt.int32
U8 = mybir.dt.uint8
ALU = mybir.AluOpType
ACT = mybir.ActivationFunctionType
AX = mybir.AxisListType

P = 128
H = 256
KC = H // P
KEYS = 77
HG = 8
HB = 4
GROWS = HG * KEYS
TILES = -(-GROWS // P)
TROWS = [min(P, GROWS - j * P) for j in range(TILES)]
TFIRST = [j * P // KEYS for j in range(TILES)]
TLAST = [(j * P + TROWS[j] - 1) // KEYS for j in range(TILES)]
TSLOT = [sum(TLAST[i] - TFIRST[i] + 1 for i in range(j)) for j in range(TILES + 1)]
PAIR = 2
LANES = 4
NEG = -float(2 ** 100)
EPS = 1e-5
CH = 16
ST = 64


class Attn:

    def __init__(self, name, heads, hd):
        self.name, self.heads, self.hd = name, heads, hd
        self.width = heads * hd
        self.chunks = self.width // P
        self.hpc = P // hd
        self.cpg = HG // self.hpc
        self.halves = self.hpc > 2
        self.hpp = self.hpc // 2 if self.halves else self.hpc
        self.groups = heads // HG
        self.scale = float(hd) ** -0.5


L0, L1, L2, L3 = Attn("0", 8, 32), Attn("1", 16, 64), Attn("2", 16, 16), Attn("3", 16, 16)
ATTN = {a.name: a for a in (L0, L1, L2, L3)}


def norm_steps(key):
    return [("stats", key), ("aggr", key), ("vareps", key), ("rstd", key), ("norm", key)]


def attention_steps(a):
    if a is L1:
        steps = [("query", "1a"), ("query", "1b"), ("query_add", "1a"), ("query_add", "1b")]
    else:
        steps = [("query", a.name), ("query_bias", a.name)]
    for g in range(a.groups):
        k = f"{a.name}.{g}"
        steps += [("scores", k), ("rowmax", k)]
        if a is L2:
            steps += [("clamp", k)]
        steps += [("shift", k), ("expo", k)]
        if a is L2:
            steps += [("maskmul", k)]
        if a is L1:
            steps += [("rowsum", k), ("recip", k), ("weigh", k)]
        steps += [("pturn", k), ("pturn_main", k), ("pturn_rest", k), ("mix", k)]
        if a is L1:
            steps += [("resid", k)]
        else:
            if a is L2:
                steps += [("den_eps", k)]
            steps += [("recip", k), ("heads", k)]
    if a is not L1:
        o = a.name + "o"
        steps += [("turn", o), ("turned", o), ("proj", a.name), ("resid", a.name)]
    return steps


BEFORE = (norm_steps("0") + [("prebias", "0"), ("turn", "0"), ("turned", "0")] + attention_steps(L0)
          + norm_steps("u") + [("keep", "u"), ("turn", "u"), ("turned", "u"), ("uproj", "u"), ("u_sb", "u")])
AFTER = ([("state", "s"), ("ssm", "s"), ("resume", "s")]
         + norm_steps("1") + [("prebias", "1"), ("turn", "1"), ("turned", "1")] + attention_steps(L1)
         + [("turn", "2"), ("turned", "2"), ("prebias", "2")] + attention_steps(L2)
         + norm_steps("2") + [("gain", "2"), ("offset", "2")]
         + norm_steps("3") + [("prebias", "3"), ("turn", "3"), ("turned", "3")] + attention_steps(L3)
         + norm_steps("m") + [("prebias", "m"), ("turn", "m"), ("turned", "m"),
                              ("fc1", "ma"), ("fc1", "mb"), ("gelu", "ma"), ("gelu", "mb"), ("fc2", "ma"), ("fc2", "mb"),
                              ("resid", "m"), ("store", "m")])


MADE_BY = {
    "tensor": ("turn", "query", "scores", "pturn", "mix", "proj", "uproj", "ssm", "fc1", "fc2"),
    "scalar": ("turned", "query_bias", "expo", "pturn_main", "u_sb", "gelu"),
    "vector": ("stats", "aggr", "norm", "query_add", "rowmax", "clamp", "shift", "rowsum", "den_eps", "recip", "weigh",
               "pturn_rest", "heads", "resid", "resume"),
    "gpsimd": ("vareps", "rstd", "prebias", "keep", "state", "maskmul", "gain", "offset"),
    "sync": ("store",)}
TURNS = [
    {"tensor": "102103120312103102102302323310123023",
     "vector": "110202130233110012211033002112231000331202233323",
     "scalar": "1012302110302123032310231203",
     "gpsimd": "110202333011120001223323"},
    {"tensor": (
        "013201002101223123030310212102303013010121231232032301312021320301310012132322303001101203203213"
        "01202031230132121301303201231113133202202233"),
     "vector": (
        "000111031222303201300100202112201321312023130203100032301123110132123231232303320013110222010033"
        "312110020221311203233000123313110002103121220033130221213331230022332030011002120332010122311233"
        "20010323110311233121332223312203"),
     "scalar": "0120310213200310120312130221303212303101203123230010102321301202303121231302311103032322",
     "gpsimd": "01320011221033230101232301230000110011021132323232233100021313232312",
     "sync": "0123"},
]


def in_turn(plan, engine, lanes):
    own = [(s, k) for s, k in plan if s in MADE_BY[engine]]
    at, out = [0] * LANES, []
    for lane in map(int, lanes):
        out.append((*own[at[lane]], lane))
        at[lane] += 1
    assert at == [len(own)] * LANES
    return out


FREED = {"tensor": (("turn", 0), ("scores", 1), ("ssm", 1)), "scalar": (("u_sb", 0),), "vector": (("resid", 1),)}


class Counts:

    def __init__(self, iters):
        self.iters = iters
        self.order = [{e: in_turn(plan, e, TURNS[ph].get(e, "")) for e in MADE_BY}
                      for ph, plan in enumerate((BEFORE, AFTER))]
        self.per = [{}, {}]
        self.index = [{}, {}]
        for ph, order in enumerate(self.order):
            for s, k, lane in (step for steps in order.values() for step in steps):
                self.index[ph][s, k, lane] = self.per[ph].get(s, 0)
                self.per[ph][s] = self.per[ph].get(s, 0) + 1
        self.steps = sorted((set(self.per[0]) | set(self.per[1])) - {"store"})
        self.start = {s: self.per[ph][s] for steps in FREED.values() for s, ph in steps}

    def before_loop(self, ph, pair, step):
        a, b = (self.iters * self.per[q].get(step, 0) for q in (0, 1))
        return pair * (a + b) + (a if ph else 0) + self.start.get(step, 0)

    def tick(self, ph, pair, i):
        return Tick(self, ph, pair, i)


class Tick:

    def __init__(self, counts, ph, pair, i):
        self.c, self.ph, self.pair, self.i = counts, ph, pair, i

    def done(self, step, key, lane):
        c, ph = self.c, self.ph
        return c.before_loop(ph, self.pair, step) + self.i * c.per[ph][step] + c.index[ph][step, key, lane] + 1

    def earlier(self, step, key, lane):
        return self.done(step, key, lane) - self.c.per[self.ph][step]


def xattn_chain(nc, A):
    out = A["out"]
    B, S, _ = A["x"].shape
    NT = S // P
    TPL = LANES // PAIR
    ITERS = NT // TPL
    NCH = S // CH
    PAIRS = B // PAIR
    HID = A["L3_xattn_fc1_w"].shape[1]
    NH = HID // P
    PK = PAIR * KEYS
    counts = Counts(ITERS)

    with ExitStack() as ctx:
        def sb(name, shape, dt=F32):
            return ctx.enter_context(nc.sbuf_tensor(name, shape, dt))

        sems = {}

        def sem(name):
            sems[name] = ctx.enter_context(nc.semaphore(name))
            return sems[name]

        wT = {"0": sb("wT0", [P, KC, 4 * H]), "2": sb("wT2", [P, KC, 4 * H])}
        wq1 = sb("wq1", [P, KC, L1.width])
        wq3 = sb("wq3", [P, KC, H])
        wp3 = sb("wp3", [P, KC, H])
        wkv3 = sb("wkv3", [P, KC, 2 * H])
        wo1 = sb("wo1", [P, L1.chunks, H])
        fc1 = sb("fc1", [P, KC, HID])
        fc2 = sb("fc2", [P, NH, H])
        wU = sb("wU", [P, KC, ST])
        cmat = sb("cmat", [ST, H])
        aT = sb("aT", [ST, ST])
        wprogT = sb("wprogT", [ST, H])
        def cols(name, n):
            return sb(name, [P, n])
        g0, be0, gu, beu = cols("g0", KC), cols("be0", KC), cols("gu", KC), cols("beu", KC)
        g1, be1, g3, be3 = cols("g1", KC), cols("be1", KC), cols("g3", KC), cols("be3", KC)
        gc, bec, gm, bem = cols("gc", KC), cols("bec", KC), cols("gm", KC), cols("bem", KC)
        bqk0, bq1, bkv1 = cols("bqk0", 2 * KC), cols("bq1", L1.chunks), cols("bkv1", 2 * L1.chunks)
        bq2, bk2, bfc1, bin_ = cols("bq2", KC), cols("bk2", KC), cols("bfc1", NH), cols("bin_", KC)
        bU = sb("bU", [ST, 1])
        row_names = ["bo0", "bo1", "bo2", "g2", "be2", "bp3", "bfc2", "bv0", "bv2", "bprog"]
        rows = {n: sb("row_" + n, [P, H]) for n in row_names}
        modrow = sb("modrow", [P, PAIR, H])
        kblk = {a.name: sb("kblk" + a.name, [P, PAIR, a.chunks, a.hpp, KEYS]) for a in ATTN.values()}
        vtab = {a.name: sb("vtab" + a.name, [P, PAIR, a.groups, TSLOT[-1], a.hd + 1]) for a in (L0, L2, L3)}
        vwo = sb("vwo", [P, PAIR, L1.groups, TILES, H])
        neg3 = sb("neg3", [P, PAIR, NT, KEYS], BF16)
        neg2 = sb("neg2", [P, NT, KEYS], BF16)
        mul2 = sb("mul2", [P, NT, KEYS])
        causal = sb("causal", [P, NT, KEYS], BF16)
        ident = sb("ident", [P, P])
        identb = sb("identb", [P, P], BF16)
        hmask = {a.hd: sb(f"hmask{a.hd}", [P, a.hpc]) for a in (L0, L1, L2)}
        halfmask = {a.hd: sb(f"halfmask{a.hd}", [P, a.hpp]) for a in (L0, L2)}
        tmask = sb("tmask", [P, TILES, HG])
        smask = sb("smask", [P, TSLOT[-1]])
        ones1 = sb("ones1", [1, P])
        mean77 = sb("mean77", [P, 1])
        halfneg = sb("halfneg", [P, 1])
        scan = sb("scan", [P, 2, PAIR * (S + 1)])
        U = scan[0:ST, 0, :].rearrange("p (b t) -> p b t", b=PAIR)
        R = scan[0:ST, 1, :].rearrange("p (b t) -> p b t", b=PAIR)
        NC1 = L1.chunks
        CROWS = L1.hpc * KEYS
        GC = NC1 // L1.groups
        WIDE = 2 * P
        FROM = [(c * CROWS // P) * P - c * CROWS for c in range(GC)]
        vtw = scan[:, :, :].rearrange("p a n -> p (a n)")[:, 0:PAIR * NC1 * WIDE].rearrange(
            "p (b c n) -> p b c n", b=PAIR, c=NC1)
        ends = sb("ends", [ST, PAIR, NCH])
        gap = sb("gap", [ST, 2])
        gmx = sb("gmx", [1, 3])
        agree = sb("agree", [1, 1], I32)
        xs = sb("xs", [P, PAIR, NT, H])
        x = sb("xt", [P, LANES, H])
        z = sb("zt", [P, LANES, H])
        t = sb("tt", [P, LANES, KC, P])
        big = sb("big", [P, LANES, HID])
        pr = sb("pr", [P, LANES, 5 * P])
        stat = sb("stat", [P, LANES, 6])
        mv = sb("mv", [P, LANES, 2])
        rstd = sb("rstd", [P, LANES])
        mx = sb("mx", [P, LANES, HG])
        rec = sb("rec", [P, LANES, HG])
        wkv1 = big[:, :, :].rearrange("p l n -> p (l n)").rearrange("p (k n) -> p k n", k=KC)
        cz = x[0:KEYS, 0:PAIR, :]
        ct1 = t[:, :, :, :].rearrange("p l c n -> p (l c n)")[:, 0:KC * PK].rearrange("p (c n) -> p c n", c=KC)
        xflat = xs[:, :, :, :].rearrange("p b t n -> p (b t n)")
        ct3 = {n: xflat[:, k * KC * 3 * PK:(k + 1) * KC * 3 * PK].rearrange("p (c b r n) -> p c b r n", c=KC, b=PAIR, r=3)
               for k, n in enumerate("023")}
        cstat = sb("cstat", [KEYS, PAIR, 6])
        cmv = sb("cmv", [KEYS, PAIR, 2])
        crs = sb("crs", [KEYS, PAIR])
        ktmp = sb("ktmp", [P, 2, PK])
        cx = sb("cx", [KEYS, PAIR, H])
        cb = sb("cb", [KEYS, PAIR, ST])
        m3raw = sb("m3raw", [P, PAIR, NT, KEYS], U8)
        mT = sb("mT", [ST, PAIR])
        stage = xs[:, :, :, :].rearrange("p b t n -> p (b t) n")
        win = big[:, 0, 0:KC * H].rearrange("p (c n) -> p c n", c=KC)
        bmat = big[:, 1, 0:KC * ST].rearrange("p (c n) -> p c n", c=KC)
        wprog = big[:, 1, 256:256 + KC * ST].rearrange("p (c n) -> p c n", c=KC)
        araw = big[0:ST, 1, 512:512 + ST]
        m2i = z[:, :, :].rearrange("p l n -> p (l n)")[:, 0:NT * KEYS].bitcast(I32).rearrange(
            "p (t k) -> p t k", t=NT)

        ps = ctx.enter_context(nc.psum_tensor("ps", [P, 8, 512], F32))

        done = {s: sem(s + "_done") for s in counts.steps}
        stored = [sem(f"stored{lane}") for lane in range(LANES)]
        stage_in = sem("stage_in")
        weights_in = sem("weights_in")
        late_in = sem("late_in")
        consts = sem("consts")
        masks2 = sem("masks2")
        setup_mm, setup_ev = sem("setup_mm"), sem("setup_ev")
        ctx_in = sem("ctx_in")
        tabw_in = sem("tabw_in")
        x_in = sem("x_in")
        ctx_norm = sem("ctx_norm")
        ctx_rstd = sem("ctx_rstd")
        ctx_z = sem("ctx_z")
        tab_mm, tab_act, tab_dve = sem("tab_mm"), sem("tab_act"), sem("tab_dve")
        tab_exp = sem("tab_exp")
        vt_zero, neg3_set = sem("vt_zero"), sem("neg3_set")
        scan_zero, scan_mm, scan_r = sem("scan_zero"), sem("scan_mm"), sem("scan_r")
        ends_kept, gap_set, gap_mm, gap_row, agreed = (
            sem("ends_kept"), sem("gap_set"), sem("gap_mm"), sem("gap_row"), sem("agreed"))
        more_mm, more_r = sem("more_mm"), sem("more_r")
        states_set = sem("states_set")
        passed = {e: sem("passed_" + e) for e in ("pe", "act", "dve", "pool", "sp")}
        const_step = sem("const_step")

        ROWBLOCKS = [(n, ("0" if n < 8 else "2"), n % 8) for n in range(16)]
        NSETUP = len(ROWBLOCKS) + 3

        def k_weights(a, kc, c):
            if a is L1:
                return wkv1[:, kc, c * P:(c + 1) * P]
            if a is L3:
                return wkv3[:, kc, c * P:(c + 1) * P]
            return wT[a.name][:, kc, H + c * P:H + (c + 1) * P]

        def v_weights(a, kc):
            if a is L3:
                return wkv3[:, kc, H:2 * H]
            return wT[a.name][:, kc, 2 * H:3 * H]

        def k_ctx(a, kc):
            return ct1[:, kc, :] if a is L1 else ct3[a.name][:, kc, :, 0, :]

        k_bias = {"0": lambda c: bqk0[:, KC + c:KC + c + 1], "1": lambda c: bkv1[:, c:c + 1],
                  "2": lambda c: bk2[:, c:c + 1]}
        ITEMS = [("turnz",), ("turnz3",), ("turnraw",)]
        ITEMS += [("k", a, c) for a in (L0, L3, L2) for c in range(a.chunks)]
        ITEMS += [("mean",), ("mod", 0), ("mod", 1)]
        values = [("v", a, b) for a in (L0, L2, L3) for b in range(PAIR)]
        for n, it in enumerate([("k", L1, c) for c in range(NC1)] + [("vt", c) for c in range(NC1)]):
            ITEMS += [it]
            if n >= 1 and (n - 1) % 2 == 0 and values:
                ITEMS += [values.pop(0)]
        assert not values
        ITEMS += [("vwo", b, g, j) for b in range(PAIR) for g in range(L1.groups) for j in range(TILES)]
        ON_DVE = {"turnz3", "turnraw", "mod", "v", "vwo"}
        act_no, dve_no, k_no = {}, {}, {}
        for n, it in enumerate(ITEMS):
            (dve_no if it[0] in ON_DVE else act_no)[it] = len(dve_no if it[0] in ON_DVE else act_no)
            if it[0] == "k":
                k_no[it] = len(k_no)
        V_DONE = max(dve_no[it] for it in dve_no if it[0] == "v") + 1
        NACT, NDVE, NK, NI = len(act_no), len(dve_no), len(k_no), len(ITEMS)
        BANKS = 8

        def bank(lane, k):
            return ps[:, 2 * lane + k, :]

        def banks(lane):
            return ps[:, 2 * lane:2 * lane + 2, :]

        def half_of(key, chunks):
            first = {"a": 0, "b": chunks // 2}
            return range(first[key[-1]], first[key[-1]] + chunks // 2) if key[-1] in first else range(chunks)

        def stores(pair, i):
            return (pair * ITERS + i) * 16 + 1

        def tile_of(lane, tick):
            return lane % PAIR, tick.i * TPL + lane // PAIR

        def chunk_view(ap2):
            return ap2.rearrange("p b (c l) -> p b c l", l=CH)

        block = ctx.enter_context(nc.Block())

        col_loads = [(g0, "L0_xattn_g1"), (be0, "L0_xattn_beta1"), (gu, "L0_xattn_g2"), (beu, "L0_xattn_beta2"),
                     (g1, "L1_xattn_ln_g"), (be1, "L1_xattn_ln_b"), (g3, "L3_xattn_qn_w"), (be3, "L3_xattn_qn_b"),
                     (gc, "L3_xattn_cn_w"), (bec, "L3_xattn_cn_b"), (gm, "L3_xattn_n2_w"), (bem, "L3_xattn_n2_b"),
                     (bq1, "L1_xattn_bq"), (bkv1, "L1_xattn_bkv"), (bq2, "L2_xattn_bq"), (bk2, "L2_xattn_bk"),
                     (bfc1, "L3_xattn_fc1_b"), (bin_, "L0_xattn_b_in")]
        row_loads = [("bo0", A["L0_xattn_b_o"]), ("bo1", A["L1_xattn_bo"]), ("bo2", A["L2_xattn_bo"]),
                     ("g2", A["L2_xattn_ln_g"]), ("be2", A["L2_xattn_ln_b"]), ("bp3", A["L3_xattn_proj_b"]),
                     ("bfc2", A["L3_xattn_fc2_b"]), ("bv0", A["L0_xattn_b_qkv"][2 * H:3 * H]),
                     ("bv2", A["L2_xattn_bv"]), ("bprog", A["L0_xattn_b_prog"])]
        by_chunk = [(wq1, "L1_xattn_wq"), (wq3, "L3_xattn_q_w"), (wp3, "L3_xattn_proj_w"), (fc1, "L3_xattn_fc1_w"),
                    (fc2, "L3_xattn_fc2_w")]
        for_tables = [(wkv3, "L3_xattn_kv_w"), (wo1, "L1_xattn_wo")]
        NSTAGE = 6 + 5
        NWEIGHTS = len(for_tables) + len(col_loads) + 4 + len(row_loads)
        NLATE = len(by_chunk) + 1
        NCTX = 2 + PAIR

        @block.sync
        def _(sp):
            for lane in range(LANES):
                sp.sem_inc(stored[lane], 1)
            sp.dma_start(stage[:, 0:6, :], A["L0_xattn_W_qkv"].rearrange("(c p) n -> p c n", p=P)).then_inc(stage_in, 16)
            sp.dma_start(stage[:, 6:8, :], A["L0_xattn_W_o"].rearrange("(c p) n -> p c n", p=P)).then_inc(stage_in, 16)
            for n, name in enumerate(("Wq", "Wk", "Wv", "Wo")):
                sp.dma_start(stage[:, 8 + 2 * n:10 + 2 * n, :],
                             A["L2_xattn_" + name].rearrange("(c p) n -> p c n", p=P)).then_inc(stage_in, 16)
            sp.dma_start(win, A["L0_xattn_W_in"].rearrange("(c p) n -> p c n", p=P)).then_inc(stage_in, 16)
            sp.dma_start(bmat, A["L0_xattn_Bmat"].rearrange("(c p) n -> p c n", p=P)).then_inc(stage_in, 16)
            sp.dma_start(wprog, A["L0_xattn_W_prog"].rearrange("(c p) n -> p c n", p=P)).then_inc(stage_in, 16)
            sp.dma_start(araw, A["L0_xattn_A"]).then_inc(stage_in, 16)
            sp.dma_start(m2i, A["mask_1x1xSxS2_if1"][0, 0].rearrange("(t p) k -> p t k", p=P)).then_inc(stage_in, 16)
            for dst, name in for_tables:
                sp.dma_start(dst[:, :, :], A[name].rearrange("(c p) n -> p c n", p=P)).then_inc(weights_in, 16)

            def load_context(pair):
                sp.dma_start(cx[:, :, :], A["ctx_1024"][bass.ds(pair * PAIR, PAIR)].rearrange("b k n -> k b n")).then_inc(ctx_in, 16)
                sp.dma_start(cb[:, :, :], A["ctxb_2048x64"][bass.ds(pair * PAIR, PAIR)].rearrange("b k n -> k b n")).then_inc(ctx_in, 16)
                for b in range(PAIR):
                    sp.dma_start(m3raw[:, b, :, :], A["mask_BxSxS2_bk0"][bass.ds(pair * PAIR + b, 1)].rearrange(
                        "o (t p) k -> p (o t) k", p=P)).then_inc(ctx_in, 16)

            load_context(0)

            with sp.Fori(0, PAIRS) as pair:
                sp.wait_ge(done["resid"], counts.before_loop(0, pair, "resid"))
                sp.wait_ge(setup_ev, NSETUP)
                sp.dma_start(wkv1, A["L1_xattn_wkv"].rearrange("(c p) n -> p c n", p=P)).then_inc(tabw_in, 16)
                sp.wait_ge(masks2, 2)
                sp.wait_ge(tab_dve, pair * NDVE + V_DONE)
                for b in range(PAIR):
                    sp.dma_start(xs[:, b, :, :], A["x"][bass.ds(pair * PAIR + b, 1)].rearrange(
                        "o (t p) n -> p (o t) n", p=P)).then_inc(x_in, 16)
                sp.wait_ge(tab_mm, (pair + 1) * NI)
                sp.wait_ge(neg3_set, pair + 1)
                sp.sem_inc(passed["sp"], 1)
                with sp.If(pair < PAIRS - 1):
                    load_context((pair + 1) % PAIRS)
                with sp.Fori(0, ITERS) as i:
                    tick = counts.tick(1, pair, i)
                    for _, _, lane in counts.order[1]["sync"]:
                        b, tile = tile_of(lane, tick)
                        sp.wait_ge(done["resid"], tick.done("resid", "m", lane))
                        sp.dma_start(out[bass.ds(pair * PAIR + b, 1), bass.ds(tile * P, P), :].rearrange("o p n -> (o p) n"),
                                     x[:, lane, :]).then_inc(stored[lane], 16)
            for lane in range(LANES):
                sp.wait_ge(stored[lane], stores(PAIRS, 0))

        @block.tensor
        def _(pe):
            mm = nc.tensor.matmul

            for s, _ in FREED["tensor"]:
                pe.sem_inc(done[s], counts.start[s])
            pe.wait_ge(stage_in, NSTAGE * 16)
            pe.wait_ge(consts, 1)
            for n, (src, _, _) in enumerate(ROWBLOCKS):
                if n >= BANKS:
                    pe.wait_ge(setup_ev, n - BANKS + 1)
                for kc in range(KC):
                    last = nc.tensor.transpose(ps[:, n % BANKS, kc * P:(kc + 1) * P], stage[:, src, kc * P:(kc + 1) * P], ident[:, :])
                last.then_inc(setup_mm, 1)
            n = len(ROWBLOCKS)
            pe.wait_ge(setup_ev, n - BANKS + 1)
            for c in range(KC):
                last = nc.tensor.transpose(ps[0:ST, n % BANKS, c * P:(c + 1) * P], wprog[:, c, :], ident[:, :])
            last.then_inc(setup_mm, 1)
            n += 1
            pe.wait_ge(setup_ev, n - BANKS + 1)
            nc.tensor.transpose(ps[0:ST, n % BANKS, 0:ST], araw, ident[0:ST, 0:ST]).then_inc(setup_mm, 1)
            n += 1
            pe.wait_ge(setup_ev, n - BANKS + 1)
            pe.wait_ge(weights_in, NWEIGHTS * 16)
            for kc in range(KC):
                for oc in range(KC):
                    mm(ps[:, n % BANKS, kc * ST:(kc + 1) * ST], win[:, oc, kc * P:(kc + 1) * P], bmat[:, oc, :],
                       start=oc == 0, stop=oc == KC - 1)
            for oc in range(KC):
                last = mm(ps[0:ST, n % BANKS, KC * ST:KC * ST + 1], bmat[:, oc, :], bin_[:, oc:oc + 1],
                          start=oc == 0, stop=oc == KC - 1)
            last.then_inc(setup_mm, 1)

            def tables(pair):
                pe.wait_ge(setup_ev, NSETUP)
                pe.wait_ge(done["resid"], counts.before_loop(0, pair, "resid"))
                for n, it in enumerate(ITEMS):
                    if n >= BANKS:
                        old = ITEMS[n - BANKS]
                        if old[0] in ON_DVE:
                            pe.wait_ge(tab_dve, pair * NDVE + dve_no[old] + 1)
                        else:
                            pe.wait_ge(tab_act, pair * NACT + act_no[old] + 1)
                    bk = ps[:, n % BANKS, :]
                    kind = it[0]
                    if kind in ("turnz", "turnz3"):
                        pe.wait_ge(ctx_z, pair + 1)
                        for c in range(KC):
                            for b in range(PAIR):
                                o = c * PK + b * KEYS
                                last = nc.tensor.transpose(bk[:, o:o + KEYS], cz[:, b, c * P:(c + 1) * P], ident[0:KEYS, 0:KEYS])
                    elif kind == "turnraw":
                        for c in range(KC):
                            for b in range(PAIR):
                                o = c * PK + b * KEYS
                                last = nc.tensor.transpose(bk[:, o:o + KEYS], cx[:, b, c * P:(c + 1) * P], ident[0:KEYS, 0:KEYS])
                    elif kind == "k":
                        a, c = it[1:]
                        if c == 0:
                            if a in (L2, L3):
                                it = ("turnraw",) if a is L2 else ("turnz3",)
                                pe.wait_ge(tab_dve, pair * NDVE + dve_no[it] + 1)
                            else:
                                pe.wait_ge(tab_act, pair * NACT + act_no[("turnz",)] + 1)
                            if a is L1:
                                pe.wait_ge(tabw_in, (pair + 1) * 16)
                        for kc in range(KC):
                            last = mm(bk[:, 0:PK], k_weights(a, kc, c), k_ctx(a, kc), start=kc == 0, stop=kc == KC - 1)
                    elif kind == "mean":
                        for b in range(PAIR):
                            last = mm(bk[0:ST, b:b + 1], cb[:, b, :], mean77[0:KEYS, :], start=True, stop=True)
                    elif kind == "mod":
                        b = it[1]
                        pe.wait_ge(tab_act, pair * NACT + act_no[("mean",)] + 1)
                        last = mm(bk[:, 0:H], mT[:, b:b + 1].to_broadcast([ST, P]), wprogT[:, :], start=True, stop=True)
                    elif kind == "v":
                        a, b = it[1:]
                        for j in range(TILES):
                            o = bk[:, 0:TSLOT[-1] * a.groups * a.hd].rearrange("p (g n) -> p g n", g=a.groups)[
                                :, :, TSLOT[j] * a.hd:TSLOT[j + 1] * a.hd]
                            own = slice(TFIRST[j] * a.hd, (TLAST[j] + 1) * a.hd)
                            k0 = j * P % KEYS
                            for kc in range(KC):
                                keys = ct3[a.name][:, kc, b, :, :].rearrange("p r n -> p (r n)")[:, k0:k0 + P]
                                last = mm(o, keys, v_weights(a, kc).rearrange("p (g n) -> p g n", g=a.groups)[:, :, own],
                                          start=j == 0 and kc == 0, stop=a is L3 and kc == KC - 1, skip_group_check=True)
                            if a is not L3:
                                bias = rows["bv" + a.name][0:1, :].rearrange("p (g n) -> p g n", g=a.groups)[:, :, own]
                                last = mm(o, ones1[:, :], bias, start=False, stop=True, skip_group_check=True)
                    elif kind == "vt":
                        c = it[1]
                        for kc in range(KC):
                            last = mm(bk[:, 0:PK], wkv1[:, kc, L1.width + c * P:L1.width + (c + 1) * P], ct1[:, kc, :],
                                      start=kc == 0, stop=kc == KC - 1)
                    else:
                        b, g, j = it[1:]
                        pe.wait_ge(tab_act, (pair + 1) * NACT)
                        c0, c1 = j * P // CROWS, (j * P + TROWS[j] - 1) // CROWS
                        for c in range(c0, c1 + 1):
                            at = j * P - c * CROWS - FROM[c]
                            last = mm(bk[0:TROWS[j], 0:H], vtw[:, b, g * GC + c, at:at + TROWS[j]], wo1[:, g * GC + c, :],
                                      start=c == c0, stop=c == c1)
                    last.then_inc(tab_mm, 1)

            def turn(key, lane, tick):
                if key == "0":
                    pe.wait_ge(done["u_sb"], tick.earlier("u_sb", "u", lane))
                if key in ("0", "u", "1", "3", "m"):
                    pe.wait_ge(done["norm"], tick.done("norm", key, lane))
                    src = z
                elif key == "2":
                    pe.wait_ge(done["resid"], tick.done("resid", "1.1", lane))
                    src = x
                else:
                    pe.wait_ge(done["heads"], tick.done("heads", f"{key[0]}.{ATTN[key[0]].groups - 1}", lane))
                    src = z
                for c in range(KC):
                    last = nc.tensor.transpose(bank(lane, 0)[:, c * P:(c + 1) * P], src[:, lane, c * P:(c + 1) * P], ident[:, :])
                last.then_inc(done["turn"], 1)

            def query(key, lane, tick):
                a = ATTN[key[0]]
                pe.wait_ge(done["turned"], tick.done("turned", key[0], lane))
                w = {"0": wT["0"], "1": wq1, "2": wT["2"], "3": wq3}[key[0]]
                for c in half_of(key, a.chunks):
                    for kc in range(KC):
                        last = mm(bank(lane, c // 4)[:, c % 4 * P:(c % 4 + 1) * P], w[:, kc, c * P:(c + 1) * P], t[:, lane, kc, :],
                                  start=kc == 0, stop=kc == KC - 1)
                last.then_inc(done["query"], 1)

            def scores(key, lane, tick):
                a, g = ATTN[key[0]], int(key[2])
                b, tile = tile_of(lane, tick)
                if g == 0:
                    if a is L1:
                        for k in ("1a", "1b"):
                            pe.wait_ge(done["query_add"], tick.done("query_add", k, lane))
                    else:
                        pe.wait_ge(done["query_bias"], tick.done("query_bias", a.name, lane))
                elif a is L1:
                    pe.wait_ge(done["resid"], tick.done("resid", "1.0", lane))
                else:
                    pe.wait_ge(done["heads"], tick.done("heads", f"{a.name}.0", lane))
                w = a.hpp * KEYS
                masked = a is not L0 and not (a is L1 and lane // PAIR * P >= KEYS)
                for n in range(a.cpg):
                    c = g * a.cpg + n
                    if a.halves:
                        for k in range(2):
                            half = slice(k * P // 2, (k + 1) * P // 2)
                            last = mm(bank(lane, k)[:, n * w:(n + 1) * w], big[half, lane, c * P:(c + 1) * P],
                                      kblk[a.name][half, b, c, :, :], start=n == 0, stop=not masked, skip_group_check=True)
                    else:
                        k, at = divmod(n * a.hpc, HB)
                        last = mm(bank(lane, k)[:, at * KEYS:at * KEYS + w], big[:, lane, c * P:(c + 1) * P],
                                  kblk[a.name][:, b, c, :, :], start=at == 0, stop=not masked, skip_group_check=True)
                if masked:
                    m = {"1": causal[:, bass.ds(tile, 1), :], "2": neg2[:, bass.ds(tile, 1), :],
                         "3": neg3[:, b, bass.ds(tile, 1), :]}[a.name]
                    for k in range(2):
                        last = mm(bank(lane, k)[:, 0:HB * KEYS], identb[:, :], m.to_broadcast([P, HB, KEYS]),
                                  start=False, stop=True, skip_group_check=True)
                last.then_inc(done["scores"], 1)

            def pturn(key, lane, tick):
                if key[0] == "1":
                    pe.wait_ge(done["weigh"], tick.done("weigh", key, lane))
                elif key[0] == "2":
                    pe.wait_ge(done["maskmul"], tick.done("maskmul", key, lane))
                else:
                    pe.wait_ge(done["expo"], tick.done("expo", key, lane))
                for j in range(TILES):
                    last = nc.tensor.transpose(bank(lane, j // 4)[0:TROWS[j], j % 4 * P:(j % 4 + 1) * P],
                                               pr[:, lane, j * P:j * P + TROWS[j]], ident[:, :])
                last.then_inc(done["pturn"], 1)

            def mix(key, lane, tick):
                a, g = ATTN[key[0]], int(key[2])
                b, _ = tile_of(lane, tick)
                pe.wait_ge(done["pturn_main"], tick.done("pturn_main", key, lane))
                pe.wait_ge(done["pturn_rest"], tick.done("pturn_rest", key, lane))
                o = bank(lane, 0)
                for j in range(TILES):
                    pt = pr[0:TROWS[j], lane, j * P:(j + 1) * P]
                    if a is L1:
                        last = mm(o[:, 0:H], pt, vwo[0:TROWS[j], b, g, j, :], start=j == 0, stop=j == TILES - 1)
                    else:
                        w = a.hd + 1
                        last = mm(o[:, TFIRST[j] * w:(TLAST[j] + 1) * w], pt,
                                  vtab[a.name][0:TROWS[j], b, g, TSLOT[j]:TSLOT[j + 1], :],
                                  start=j == 0, stop=j == TILES - 1, skip_group_check=True)
                last.then_inc(done["mix"], 1)

            def proj(key, lane, tick):
                pe.wait_ge(done["turned"], tick.done("turned", key + "o", lane))
                for kc in range(KC):
                    w = wp3[:, kc, :] if key == "3" else wT[key][:, kc, 3 * H:4 * H]
                    last = mm(bank(lane, 1)[:, 0:H], t[:, lane, kc, :], w, start=kc == 0, stop=kc == KC - 1)
                last.then_inc(done["proj"], 1)

            def uproj(key, lane, tick):
                pe.wait_ge(done["turned"], tick.done("turned", "u", lane))
                for kc in range(KC):
                    last = mm(bank(lane, 0)[0:ST, 0:P], wU[:, kc, :], t[:, lane, kc, :], start=kc == 0, stop=kc == KC - 1)
                last.then_inc(done["uproj"], 1)

            def ssm(key, lane, tick):
                pe.wait_ge(done["state"], tick.done("state", "s", lane))
                mm(bank(lane, 0)[:, 0:H], big[0:ST, lane, 0:P], cmat[:, :], start=True, stop=True).then_inc(done["ssm"], 1)

            def do_fc1(key, lane, tick):
                pe.wait_ge(done["turned"], tick.done("turned", "m", lane))
                for c in half_of(key, NH):
                    for kc in range(KC):
                        last = mm(bank(lane, c // 4)[:, c % 4 * P:(c % 4 + 1) * P], fc1[:, kc, c * P:(c + 1) * P], t[:, lane, kc, :],
                                  start=kc == 0, stop=kc == KC - 1)
                last.then_inc(done["fc1"], 1)

            def do_fc2(key, lane, tick):
                pe.wait_ge(done["gelu"], tick.done("gelu", key, lane))
                for c in half_of(key, NH):
                    last = mm(bank(lane, 0)[:, 0:H], big[:, lane, c * P:(c + 1) * P], fc2[:, c, :], start=c == 0, stop=c == NH - 1)
                last.then_inc(done["fc2"], 1)

            def scan_step(n, l, mm_done, r_done, past):
                uin, rin = chunk_view(U[:, :, 0:S]), chunk_view(R[:, :, 0:S])
                o = ps[0:ST, l % 2, 0:PAIR * NCH]
                mm(o, aT[:, :], uin[:, :, :, l], start=True, stop=False)
                pe.wait_ge(r_done, past + n + 1)
                pe.sem_inc(passed["pe"], 1)
                mm(o, aT[:, :], rin[:, :, :, l], start=False, stop=True).then_inc(mm_done, 1)

            def scan_pair(pair):
                pe.wait_ge(done["u_sb"], counts.before_loop(1, pair, "u_sb"))
                pe.wait_ge(scan_zero, (pair + 1) * 2)
                pe.wait_ge(done["keep"], counts.before_loop(1, pair, "keep"))
                pe.sem_inc(passed["pe"], 1)
                with pe.Fori(0, 2) as sweep:
                    for l in range(CH):
                        scan_step(sweep * CH + l, l, scan_mm, scan_r, pair * 2 * CH)
                pe.wait_ge(gap_set, pair + 1)
                pe.sem_inc(passed["pe"], 1)
                for k in range(2):
                    last = nc.tensor.transpose(ps[0:1, 2, k * ST:(k + 1) * ST], gap[:, k:k + 1], ident[0:ST, 0:ST])
                last.then_inc(gap_mm, 1)
                pe.wait_ge(agreed, pair + 1)
                pe.sem_inc(passed["pe"], 1)
                ok = pe.value_load(agree[0:1, 0:1], min_val=0, max_val=1)
                more = (NCH - 2) * CH
                with pe.If(ok == 0):
                    with pe.Fori(0, NCH - 2) as sweep:
                        for l in range(CH):
                            scan_step(sweep * CH + l, l, more_mm, more_r, pair * more)
                with pe.If(ok == 1):
                    pe.sem_inc(more_mm, more)

            steps = {"turn": turn, "query": query, "scores": scores, "pturn": pturn, "mix": mix, "proj": proj,
                     "uproj": uproj, "ssm": ssm, "fc1": do_fc1, "fc2": do_fc2}
            with pe.Fori(0, PAIRS) as pair:
                tables(pair)
                pe.wait_ge(tab_dve, (pair + 1) * NDVE)
                pe.wait_ge(tab_exp, (pair + 1) * NK)
                pe.wait_ge(neg3_set, pair + 1)
                pe.sem_inc(passed["pe"], 1)
                with pe.Fori(0, ITERS) as i:
                    tick = counts.tick(0, pair, i)
                    for s, key, lane in counts.order[0]["tensor"]:
                        steps[s](key, lane, tick)
                scan_pair(pair)
                pe.wait_ge(late_in, NLATE * 16)
                with pe.Fori(0, ITERS) as i:
                    tick = counts.tick(1, pair, i)
                    for s, key, lane in counts.order[1]["tensor"]:
                        steps[s](key, lane, tick)

        @block.scalar
        def _(act):
            ac = nc.scalar.activation
            for s, _ in FREED["scalar"]:
                act.sem_inc(done[s], counts.start[s])
            act.sem_inc(scan_r, 1)
            act.sem_inc(more_r, 1)
            for dst, name in col_loads:
                act.dma_start(dst[:, :], A[name].rearrange("(c p) -> p c", p=P), allow_slow_non_contiguous=True).then_inc(weights_in, 16)
            for q in range(2):
                for k in range(2):
                    act.dma_start(bqk0[k * P // 2:(k + 1) * P // 2, q * KC:(q + 1) * KC],
                                  A["L0_xattn_b_qkv"][0:2 * H].rearrange("(q k n d) -> q k d n", q=2, k=2, d=P // 2)[q, k],
                                  allow_slow_non_contiguous=True).then_inc(weights_in, 16)
            for n, v in row_loads:
                act.dma_start(rows[n][:, :], v.partition_broadcast(P)).then_inc(weights_in, 16)
            for dst, name in by_chunk:
                act.dma_start(dst[:, :, :], A[name].rearrange("(c p) n -> p c n", p=P)).then_inc(late_in, 16)
            act.dma_start(cmat[:, :], A["L0_xattn_Cmat"]).then_inc(late_in, 16)
            act.wait_ge(weights_in, NWEIGHTS * 16)

            def tables(pair):
                for n, it in enumerate(ITEMS):
                    if it[0] in ON_DVE:
                        continue
                    bk = ps[:, n % BANKS, :]
                    act.wait_ge(tab_mm, pair * NI + n + 1)
                    kind = it[0]
                    if kind == "turnz":
                        for c in range(KC):
                            src = bk[:, c * PK:(c + 1) * PK]
                            ac(ct1[:, c, :], src, ACT.Identity, bias=be1[:, c:c + 1], scale=g1[:, c:c + 1])
                            src = src.rearrange("p (b n) -> p b n", b=PAIR).unsqueeze(2).to_broadcast([P, PAIR, 3, KEYS])
                            last = ac(ct3["0"][:, c], src, ACT.Identity, bias=be0[:, c:c + 1], scale=g0[:, c:c + 1])
                    elif kind == "k":
                        a, c = it[1:]
                        m = k_no[it]
                        if m >= 2:
                            act.wait_ge(tab_exp, pair * NK + m - 1)
                        if a is L3:
                            last = ac(ktmp[:, m % 2, :], bk[:, 0:PK], ACT.Copy)
                        else:
                            last = ac(ktmp[:, m % 2, :], bk[:, 0:PK], ACT.Identity, bias=k_bias[a.name](c))
                        last.then_inc(tab_act, 1)
                        continue
                    elif kind == "mean":
                        last = ac(mT[:, :], bk[0:ST, 0:PAIR], ACT.Copy)
                    else:
                        c = it[1]
                        act.wait_ge(vt_zero, pair + 1)
                        v = bk[:, 0:PK].rearrange("p (b k) -> p b k", b=PAIR)
                        for n2 in range(L1.hpc):
                            h = slice(n2 * L1.hd, (n2 + 1) * L1.hd)
                            at = n2 * KEYS - FROM[c % GC]
                            last = ac(vtw[h, :, c, at:at + KEYS], v[h, :, :], ACT.Identity, bias=bkv1[h, NC1 + c:NC1 + c + 1])
                    last.then_inc(tab_act, 1)

            def turned(key, lane, tick):
                act.wait_ge(done["turn"], tick.done("turn", key, lane))
                affine = {"0": (g0, be0), "u": (gu, beu), "1": (g1, be1), "3": (g3, be3), "m": (gm, bem)}
                if key in affine:
                    gain, bias = affine[key]
                    for c in range(KC):
                        last = ac(t[:, lane, c, :], bank(lane, 0)[:, c * P:(c + 1) * P], ACT.Identity,
                                  bias=bias[:, c:c + 1], scale=gain[:, c:c + 1])
                else:
                    last = ac(t[:, lane, :, :].rearrange("p c n -> p (c n)"), bank(lane, 0)[:, 0:H], ACT.Copy)
                last.then_inc(done["turned"], 1)

            def query_bias(key, lane, tick):
                act.wait_ge(done["query"], tick.done("query", key, lane))
                if key == "3":
                    last = ac(big[:, lane, 0:H], bank(lane, 0)[:, 0:H], ACT.Copy)
                else:
                    bias = bqk0 if key == "0" else bq2
                    for c in range(KC):
                        last = ac(big[:, lane, c * P:(c + 1) * P], bank(lane, 0)[:, c * P:(c + 1) * P], ACT.Identity,
                                  bias=bias[:, c:c + 1])
                last.then_inc(done["query_bias"], 1)

            def expo(key, lane, tick):
                act.wait_ge(done["shift"], tick.done("shift", key, lane))
                v = pr[:, lane, 0:HG * KEYS]
                ac(v, v, ACT.Exp, scale=ATTN[key[0]].scale).then_inc(done["expo"], 1)

            def pturn_main(key, lane, tick):
                act.wait_ge(done["pturn"], tick.done("pturn", key, lane))
                ac(pr[:, lane, 0:4 * P], bank(lane, 0), ACT.Copy).then_inc(done["pturn_main"], 1)

            def u_sb(key, lane, tick):
                b, tile = tile_of(lane, tick)
                act.wait_ge(done["uproj"], tick.done("uproj", "u", lane))
                ac(U[:, b, bass.ds(tile * P + 1, P)], bank(lane, 0)[0:ST, 0:P], ACT.Identity, bias=bU[:, :]).then_inc(done["u_sb"], 1)

            def gelu(key, lane, tick):
                act.wait_ge(done["fc1"], tick.done("fc1", key, lane))
                for c in half_of(key, NH):
                    last = ac(big[:, lane, c * P:(c + 1) * P], bank(lane, c // 4)[:, c % 4 * P:(c % 4 + 1) * P], ACT.Gelu,
                              bias=bfc1[:, c:c + 1])
                last.then_inc(done["gelu"], 1)

            def scan_step(n, l, mm_done, r_done, past):
                rout = chunk_view(R[:, :, 1:S + 1])
                act.wait_ge(mm_done, past + n + 1)
                ac(rout[:, :, :, l], ps[0:ST, l % 2, 0:PAIR * NCH].rearrange("p (b c) -> p b c", b=PAIR),
                   ACT.Silu).then_inc(r_done, 1)

            def scan_pair(pair):
                with act.Fori(0, 2) as sweep:
                    act.wait_ge(ends_kept, pair * 2 + sweep + 1)
                    for l in range(CH):
                        scan_step(sweep * CH + l, l, scan_mm, scan_r, pair * 2 * CH)
                act.wait_ge(agreed, pair + 1)
                act.sem_inc(passed["act"], 1)
                ok = act.value_load(agree[0:1, 0:1], min_val=0, max_val=1)
                more = (NCH - 2) * CH
                with act.If(ok == 0):
                    with act.Fori(0, NCH - 2) as sweep:
                        for l in range(CH):
                            scan_step(sweep * CH + l, l, more_mm, more_r, pair * more)
                with act.If(ok == 1):
                    act.sem_inc(more_r, more)

            steps = {"turned": turned, "query_bias": query_bias, "expo": expo, "pturn_main": pturn_main, "u_sb": u_sb,
                     "gelu": gelu}
            with act.Fori(0, PAIRS) as pair:
                tables(pair)
                act.wait_ge(scan_zero, (pair + 1) * 2)
                with act.Fori(0, ITERS) as i:
                    tick = counts.tick(0, pair, i)
                    for s, key, lane in counts.order[0]["scalar"]:
                        steps[s](key, lane, tick)
                scan_pair(pair)
                with act.Fori(0, ITERS) as i:
                    tick = counts.tick(1, pair, i)
                    for s, key, lane in counts.order[1]["scalar"]:
                        steps[s](key, lane, tick)

        @block.vector
        def _(dve):
            v = nc.vector
            for s, _ in FREED["vector"]:
                dve.sem_inc(done[s], counts.start[s])
            dve.sem_inc(ends_kept, 1)
            for n, (_, layer, blk) in enumerate(ROWBLOCKS):
                dve.wait_ge(setup_mm, n + 1)
                src = ps[:, n % BANKS, 0:KC * P].rearrange("p (c n) -> p c n", c=KC)
                if layer == "0" and blk < 2 * KC:
                    part, half = blk // KC, blk % KC
                    dst = wT[layer][:, :, part * H:(part + 1) * H].rearrange("p c (n k d) -> p c k n d", k=2, d=P // 2)[:, :, half]
                    v.tensor_copy(dst, src.rearrange("p c (n d) -> p c n d", d=P // 2)).then_inc(setup_ev, 1)
                else:
                    v.tensor_copy(wT[layer][:, :, blk * P:(blk + 1) * P], src).then_inc(setup_ev, 1)
            n = len(ROWBLOCKS)
            dve.wait_ge(setup_mm, n + 1)
            v.tensor_copy(wprogT[:, :], ps[0:ST, n % BANKS, 0:H]).then_inc(setup_ev, 1)
            n += 1
            dve.wait_ge(setup_mm, n + 1)
            v.tensor_copy(aT[:, :], ps[0:ST, n % BANKS, 0:ST]).then_inc(setup_ev, 1)
            n += 1
            dve.wait_ge(setup_mm, n + 1)
            v.tensor_copy(bU[:, :], ps[0:ST, n % BANKS, KC * ST:KC * ST + 1])
            v.tensor_copy(wU[:, :, :].rearrange("p c n -> p (c n)"), ps[:, n % BANKS, 0:KC * ST]).then_inc(setup_ev, 1)
            dve.wait_ge(weights_in, NWEIGHTS * 16)
            dve.wait_ge(consts, 1)
            for a in (L0, L2, L3):
                for b in range(PAIR):
                    o = vtab[a.name][:, b, :, :, a.hd]
                    v.tensor_copy(o, smask[:, :].unsqueeze(1).to_broadcast(list(o.shape)))

            def tables(pair):
                dve.wait_ge(ctx_in, (pair + 1) * NCTX * 16)
                dve.wait_ge(done["resid"], counts.before_loop(0, pair, "resid"))
                for lane in range(LANES):
                    dve.wait_ge(stored[lane], stores(pair, 0))
                for b in range(PAIR):
                    v.bn_stats(cstat[:, b, :], cx[:, b, :]).then_inc(ctx_norm, 1)
                dve.wait_ge(ctx_norm, pair * 2 * PAIR + PAIR)
                dve.sem_inc(passed["dve"], 1)
                for b in range(PAIR):
                    v.bn_aggr(cmv[:, b, :], cstat[:, b, :]).then_inc(ctx_norm, 1)
                dve.wait_ge(ctx_rstd, pair * 2 + 2)
                for b in range(PAIR):
                    last = v.tensor_scalar(cz[:, b, :], cx[:, b, :], cmv[:, b, 0:1], crs[:, b:b + 1], ALU.subtract, ALU.mult)
                last.then_inc(ctx_z, 1)
                for n, it in enumerate(ITEMS):
                    kind = it[0]
                    bk = ps[:, n % BANKS, :]
                    if kind == "k":
                        a, c = it[1:]
                        own = halfmask[a.hd] if a.halves else hmask[a.hd]
                        m = k_no[it]
                        dve.wait_ge(tab_act, pair * NACT + act_no[it] + 1)
                        for b in range(PAIR):
                            last = v.tensor_tensor(
                                kblk[a.name][:, b, c, :, :],
                                ktmp[:, m % 2, b * KEYS:(b + 1) * KEYS].unsqueeze(1).to_broadcast([P, a.hpp, KEYS]),
                                own[:, :].unsqueeze(2).to_broadcast([P, a.hpp, KEYS]), ALU.mult)
                        last.then_inc(tab_exp, 1)
                        continue
                    if kind not in ON_DVE:
                        continue
                    dve.wait_ge(tab_mm, pair * NI + n + 1)
                    if kind == "turnz3":
                        for c in range(KC):
                            src = bk[:, c * PK:(c + 1) * PK].rearrange("p (b n) -> p b n", b=PAIR).unsqueeze(2)
                            last = v.tensor_scalar(ct3["3"][:, c], src.to_broadcast([P, PAIR, 3, KEYS]), gc[:, c:c + 1], bec[:, c:c + 1],
                                                   ALU.mult, ALU.add)
                    elif kind == "turnraw":
                        for c in range(KC):
                            src = bk[:, c * PK:(c + 1) * PK].rearrange("p (b n) -> p b n", b=PAIR).unsqueeze(2)
                            last = v.tensor_copy(ct3["2"][:, c], src.to_broadcast([P, PAIR, 3, KEYS]))
                    elif kind == "mod":
                        last = v.tensor_tensor(modrow[:, it[1], :], bk[:, 0:H], rows["bprog"][:, :], ALU.add)
                    elif kind == "v":
                        a, b = it[1:]
                        o = vtab[a.name][:, b, :, :, 0:a.hd]
                        last = v.tensor_tensor(
                            o, bk[:, 0:TSLOT[-1] * a.groups * a.hd].rearrange("p (g s d) -> p g s d", g=a.groups, d=a.hd),
                            smask[:, :].unsqueeze(1).unsqueeze(3).to_broadcast(list(o.shape)), ALU.mult)
                    else:
                        b, g, j = it[1:]
                        last = v.tensor_copy(vwo[0:TROWS[j], b, g, j, :], bk[0:TROWS[j], 0:H])
                    last.then_inc(tab_dve, 1)

            def src_of(key, lane, tick):
                if key == "0":
                    b, tile = tile_of(lane, tick)
                    return xs[:, b, bass.ds(tile, 1), :].rearrange("p o n -> p (o n)")
                return x[:, lane, :]

            def stats(key, lane, tick):
                before = {"u": ("resid", "0"), "1": ("resume", "s"), "2": ("resid", "2"), "3": ("offset", "2"), "m": ("resid", "3")}
                if key in before:
                    s, k = before[key]
                    dve.wait_ge(done[s], tick.done(s, k, lane))
                v.bn_stats(stat[:, lane, :], src_of(key, lane, tick)).then_inc(done["stats"], 1)

            def aggr(key, lane, tick):
                dve.wait_ge(done["stats"], tick.done("stats", key, lane))
                dve.sem_inc(passed["dve"], 1)
                v.bn_aggr(mv[:, lane, :], stat[:, lane, :]).then_inc(done["aggr"], 1)

            def norm(key, lane, tick):
                if key == "0":
                    dve.wait_ge(done["turn"], tick.earlier("turn", "u", lane))
                dve.wait_ge(done["rstd"], tick.done("rstd", key, lane))
                v.tensor_scalar(z[:, lane, :], src_of(key, lane, tick), mv[:, lane, 0:1], rstd[:, lane:lane + 1],
                                ALU.subtract, ALU.mult).then_inc(done["norm"], 1)

            def query_add(key, lane, tick):
                dve.wait_ge(done["query"], tick.done("query", key, lane))
                own = half_of(key, L1.chunks)
                v.tensor_tensor(big[:, lane, own[0] * P:(own[-1] + 1) * P].rearrange("p (c n) -> p c n", n=P),
                                bank(lane, own[0] // 4).rearrange("p (c n) -> p c n", n=P),
                                bq1[:, own[0]:own[-1] + 1].unsqueeze(2).to_broadcast([P, len(own), P]), ALU.add).then_inc(done["query_add"], 1)

            def score_view(lane):
                return banks(lane)[:, :, 0:HB * KEYS].rearrange("p k (h n) -> p k h n", n=KEYS)

            def rowmax(key, lane, tick):
                dve.wait_ge(done["scores"], tick.done("scores", key, lane))
                v.tensor_reduce(mx[:, lane, :].rearrange("p (k h) -> p k h", k=2), score_view(lane), AX.X, ALU.max)\
                    .then_inc(done["rowmax"], 1)

            def clamp(key, lane, tick):
                dve.wait_ge(done["rowmax"], tick.done("rowmax", key, lane))
                v.tensor_scalar(mx[:, lane, :], mx[:, lane, :], -1e9 / L2.scale, None, ALU.max).then_inc(done["clamp"], 1)

            def shift(key, lane, tick):
                s = "clamp" if key[0] == "2" else "rowmax"
                dve.wait_ge(done[s], tick.done(s, key, lane))
                p8 = pr[:, lane, 0:HG * KEYS].rearrange("p (k h n) -> p k h n", k=2, n=KEYS)
                v.tensor_tensor(p8, score_view(lane),
                                mx[:, lane, :].rearrange("p (k h) -> p k h", k=2).unsqueeze(3).to_broadcast([P, 2, HB, KEYS]),
                                ALU.subtract).then_inc(done["shift"], 1)

            def rowsum(key, lane, tick):
                dve.wait_ge(done["expo"], tick.done("expo", key, lane))
                v.tensor_reduce(mx[:, lane, :], pr[:, lane, 0:HG * KEYS].rearrange("p (h n) -> p h n", n=KEYS), AX.X, ALU.add)\
                    .then_inc(done["rowsum"], 1)

            def mixed(key, lane):
                a = ATTN[key[0]]
                return bank(lane, 0)[:, 0:HG * (a.hd + 1)].rearrange("p (h d) -> p h d", d=a.hd + 1)

            def den_eps(key, lane, tick):
                dve.wait_ge(done["mix"], tick.done("mix", key, lane))
                v.tensor_scalar(mx[:, lane, :].unsqueeze(2), mixed(key, lane)[:, :, L2.hd:L2.hd + 1], 1e-9, None, ALU.add)\
                    .then_inc(done["den_eps"], 1)

            def recip(key, lane, tick):
                if key[0] == "1":
                    dve.wait_ge(done["rowsum"], tick.done("rowsum", key, lane))
                    src = mx[:, lane, :]
                elif key[0] == "2":
                    dve.wait_ge(done["den_eps"], tick.done("den_eps", key, lane))
                    src = mx[:, lane, :]
                else:
                    dve.wait_ge(done["mix"], tick.done("mix", key, lane))
                    hd = ATTN[key[0]].hd
                    src = mixed(key, lane)[:, :, hd:hd + 1].rearrange("p h o -> p (h o)")
                v.reciprocal(rec[:, lane, :], src).then_inc(done["recip"], 1)

            def weigh(key, lane, tick):
                dve.wait_ge(done["recip"], tick.done("recip", key, lane))
                p8 = pr[:, lane, 0:HG * KEYS].rearrange("p (h n) -> p h n", n=KEYS)
                v.tensor_tensor(p8, p8, rec[:, lane, :].unsqueeze(2).to_broadcast([P, HG, KEYS]), ALU.mult).then_inc(done["weigh"], 1)

            def pturn_rest(key, lane, tick):
                dve.wait_ge(done["pturn"], tick.done("pturn", key, lane))
                v.tensor_copy(pr[0:TROWS[-1], lane, 4 * P:5 * P], bank(lane, 1)[0:TROWS[-1], 0:P]).then_inc(done["pturn_rest"], 1)

            def heads(key, lane, tick):
                a, g = ATTN[key[0]], int(key[2])
                dve.wait_ge(done["recip"], tick.done("recip", key, lane))
                w = HG * a.hd
                v.tensor_tensor(z[:, lane, g * w:(g + 1) * w].rearrange("p (h d) -> p h d", d=a.hd),
                                mixed(key, lane)[:, :, 0:a.hd],
                                rec[:, lane, :].unsqueeze(2).to_broadcast([P, HG, a.hd]), ALU.mult).then_inc(done["heads"], 1)

            def resid(key, lane, tick):
                if key[0] == "1":
                    dve.wait_ge(done["mix"], tick.done("mix", key, lane))
                    src = bank(lane, 0)
                    if key[2] == "0":
                        dve.wait_ge(done["prebias"], tick.done("prebias", "1", lane))
                    else:
                        dve.wait_ge(done["resid"], tick.done("resid", "1.0", lane))
                else:
                    dve.wait_ge(done["prebias"], tick.done("prebias", key, lane))
                    s, k = ("fc2", "mb") if key == "m" else ("proj", key)
                    dve.wait_ge(done[s], tick.done(s, k, lane))
                    src = bank(lane, 0 if key == "m" else 1)
                v.tensor_tensor(x[:, lane, :], x[:, lane, :], src[:, 0:H], ALU.add).then_inc(done["resid"], 1)

            def resume(key, lane, tick):
                b, tile = tile_of(lane, tick)
                dve.wait_ge(done["ssm"], tick.done("ssm", "s", lane))
                dve.wait_ge(stored[lane], stores(tick.pair, tick.i))
                v.tensor_tensor(x[:, lane, :], xs[:, b, bass.ds(tile, 1), :].rearrange("p o n -> p (o n)"),
                                bank(lane, 0)[:, 0:H], ALU.add).then_inc(done["resume"], 1)

            def scan_pair(pair):
                ends_now = chunk_view(R[:, :, 1:S + 1])[:, :, :, CH - 1]
                dve.wait_ge(scan_r, pair * 2 * CH + CH + 1)
                v.tensor_copy(ends[:, :, :], ends_now).then_inc(ends_kept, 1)
                dve.wait_ge(scan_r, (pair + 1) * 2 * CH + 1)
                dve.wait_ge(ends_kept, pair * 2 + 2)
                v.tensor_reduce(gap[:, 1:2], ends_now, AX.XY, ALU.max, apply_absolute_value=True)
                v.tensor_tensor(ends[:, :, :], ends[:, :, :], ends_now, ALU.subtract).then_inc(ends_kept, 1)
                dve.wait_ge(ends_kept, pair * 2 + 3)
                v.tensor_reduce(gap[:, 0:1], ends[:, :, :], AX.XY, ALU.max, apply_absolute_value=True).then_inc(gap_set, 1)
                dve.wait_ge(gap_mm, pair + 1)
                v.tensor_reduce(gmx[:, 0:2], ps[0:1, 2, 0:2 * ST].rearrange("p (k n) -> p k n", k=2), AX.X, ALU.max).then_inc(gap_row, 1)
                dve.wait_ge(gap_row, pair * 2 + 1)
                v.tensor_scalar(gmx[:, 2:3], gmx[:, 1:2], 2.0 ** -20, None, ALU.mult).then_inc(gap_row, 1)
                dve.wait_ge(gap_row, pair * 2 + 2)
                v.tensor_tensor(agree[:, :], gmx[:, 0:1], gmx[:, 2:3], ALU.is_le).then_inc(agreed, 1)
                dve.wait_ge(more_r, (pair + 1) * (NCH - 2) * CH + 1)
                v.tensor_tensor(R[:, :, 1:S + 1], R[:, :, 1:S + 1], U[:, :, 1:S + 1], ALU.add).then_inc(states_set, 1)

            steps = {"stats": stats, "aggr": aggr, "norm": norm, "query_add": query_add, "rowmax": rowmax, "clamp": clamp,
                     "shift": shift, "rowsum": rowsum, "den_eps": den_eps, "recip": recip, "weigh": weigh,
                     "pturn_rest": pturn_rest, "heads": heads, "resid": resid, "resume": resume}
            with dve.Fori(0, PAIRS) as pair:
                tables(pair)
                dve.wait_ge(x_in, (pair + 1) * PAIR * 16)
                dve.sem_inc(passed["dve"], 1)
                with dve.Fori(0, ITERS) as i:
                    tick = counts.tick(0, pair, i)
                    for s, key, lane in counts.order[0]["vector"]:
                        steps[s](key, lane, tick)
                scan_pair(pair)
                with dve.Fori(0, ITERS) as i:
                    tick = counts.tick(1, pair, i)
                    for s, key, lane in counts.order[1]["vector"]:
                        steps[s](key, lane, tick)

        @block.gpsimd
        def _(pool):
            p = nc.gpsimd
            n = [0]

            def made(ins):
                ins.then_inc(const_step, 1)
                n[0] += 1
                pool.wait_ge(const_step, n[0])

            made(p.memset(ident[:, :], 0.0))
            made(p.affine_select(out=ident[:, :], in_=ident[:, :], compare_op=ALU.not_equal, fill=1.0, base=0,
                                 pattern=[[-1, P]], channel_multiplier=1))
            made(p.tensor_copy(identb[:, :], ident[:, :]))
            masks = [(hmask[a.hd][:, :], a.hd, a.hpc) for a in (L0, L1, L2)]
            for m, d, h in masks:
                made(p.memset(m, 1.0))
                made(p.affine_select(out=m, in_=m, compare_op=ALU.is_ge, fill=0.0, base=0, pattern=[[-d, h]], channel_multiplier=1))
                made(p.affine_select(out=m, in_=m, compare_op=ALU.is_ge, fill=0.0, base=d - 1, pattern=[[d, h]], channel_multiplier=-1))
            made(p.memset(tmask[:, :, :], 1.0))
            made(p.affine_select(out=tmask[:, :, :], in_=tmask[:, :, :], compare_op=ALU.is_ge, fill=0.0, base=0,
                                 pattern=[[P, TILES], [-KEYS, HG]], channel_multiplier=1))
            made(p.affine_select(out=tmask[:, :, :], in_=tmask[:, :, :], compare_op=ALU.is_ge, fill=0.0, base=KEYS - 1,
                                 pattern=[[-P, TILES], [KEYS, HG]], channel_multiplier=-1))
            for a in (L0, L2):
                m = hmask[a.hd]
                made(p.tensor_tensor(halfmask[a.hd][:, :], m[:, 0:a.hpp], m[:, a.hpp:a.hpc], ALU.add))
            for j in range(TILES):
                made(p.tensor_copy(smask[:, TSLOT[j]:TSLOT[j + 1]], tmask[:, j, TFIRST[j]:TLAST[j] + 1]))
            made(p.memset(ones1[:, :], 1.0))
            made(p.memset(mean77[:, :], 1.0 / KEYS))
            made(p.memset(halfneg[:, :], -0.5))
            made(p.memset(causal[:, :, :], 0.0))
            p.affine_select(out=causal[:, :, :], in_=causal[:, :, :], compare_op=ALU.is_ge, fill=NEG, base=0,
                            pattern=[[P, NT], [-1, KEYS]], channel_multiplier=1).then_inc(consts, 1)
            pool.wait_ge(stage_in, NSTAGE * 16)
            p.tensor_copy(mul2[:, :, :], m2i).then_inc(masks2, 1)
            pool.wait_ge(masks2, 1)
            p.tensor_scalar(neg2[:, :, :], mul2[:, :, :], 0.0, NEG, ALU.is_equal, ALU.mult).then_inc(masks2, 1)
            pool.wait_ge(weights_in, NWEIGHTS * 16)

            def tables(pair):
                pool.wait_ge(ctx_norm, (pair + 1) * 2 * PAIR)
                pool.sem_inc(passed["pool"], 1)
                p.tensor_scalar(crs[:, :].unsqueeze(2), cmv[:, :, 1:2], EPS, None, ALU.add).then_inc(ctx_rstd, 1)
                pool.wait_ge(ctx_rstd, pair * 2 + 1)
                pool.sem_inc(passed["pool"], 1)
                p.tensor_tensor(crs[:, :], crs[:, :], halfneg[0:KEYS, :].to_broadcast([KEYS, PAIR]), ALU.pow).then_inc(ctx_rstd, 1)
                pool.wait_ge(done["ssm"], counts.before_loop(0, pair, "ssm"))
                pool.sem_inc(passed["pool"], 1)
                p.memset(vtw, 0.0).then_inc(vt_zero, 1)
                pool.wait_ge(ctx_in, (pair + 1) * NCTX * 16)
                pool.wait_ge(done["scores"], counts.before_loop(0, pair, "scores"))
                pool.sem_inc(passed["pool"], 1)
                p.tensor_scalar(neg3[:, :, :, :], m3raw[:, :, :, :], NEG, None, ALU.mult).then_inc(neg3_set, 1)
                pool.wait_ge(tab_dve, (pair + 1) * NDVE)
                pool.sem_inc(passed["pool"], 1)
                p.memset(U[:, :, 0:1], 0.0).then_inc(scan_zero, 1)
                p.memset(chunk_view(R[:, :, 0:S])[:, :, :, 0], 0.0).then_inc(scan_zero, 1)

            def vareps(key, lane, tick):
                pool.wait_ge(done["aggr"], tick.done("aggr", key, lane))
                pool.sem_inc(passed["pool"], 1)
                p.tensor_scalar(rstd[:, lane:lane + 1], mv[:, lane, 1:2], EPS, None, ALU.add).then_inc(done["vareps"], 1)

            def do_rstd(key, lane, tick):
                pool.wait_ge(done["vareps"], tick.done("vareps", key, lane))
                pool.sem_inc(passed["pool"], 1)
                r = rstd[:, lane:lane + 1]
                p.tensor_tensor(r, r, halfneg[:, :], ALU.pow).then_inc(done["rstd"], 1)

            def prebias(key, lane, tick):
                row = rows[{"0": "bo0", "1": "bo1", "2": "bo2", "3": "bp3", "m": "bfc2"}[key]]
                src = x[:, lane, :]
                if key == "2":
                    pool.wait_ge(done["turn"], tick.done("turn", "2", lane))
                else:
                    pool.wait_ge(done["norm"], tick.done("norm", key, lane))
                if key == "0":
                    b, tile = tile_of(lane, tick)
                    src = xs[:, b, bass.ds(tile, 1), :].rearrange("p o n -> p (o n)")
                pool.sem_inc(passed["pool"], 1)
                p.tensor_tensor(x[:, lane, :], src, row[:, :], ALU.add).then_inc(done["prebias"], 1)

            def keep(key, lane, tick):
                b, tile = tile_of(lane, tick)
                pool.wait_ge(done["resid"], tick.done("resid", "0", lane))
                pool.sem_inc(passed["pool"], 1)
                p.tensor_tensor(xs[:, b, bass.ds(tile, 1), :].rearrange("p o n -> p (o n)"), x[:, lane, :], modrow[:, b, :],
                                ALU.add).then_inc(done["keep"], 1)

            def state(key, lane, tick):
                b, tile = tile_of(lane, tick)
                pool.wait_ge(done["resid"], tick.earlier("resid", "m", lane))
                pool.sem_inc(passed["pool"], 1)
                p.tensor_copy(big[0:ST, lane, 0:P], R[:, b, bass.ds(tile * P + 1, P)]).then_inc(done["state"], 1)

            def maskmul(key, lane, tick):
                _, tile = tile_of(lane, tick)
                pool.wait_ge(done["expo"], tick.done("expo", key, lane))
                pool.sem_inc(passed["pool"], 1)
                p8 = pr[:, lane, 0:HG * KEYS].rearrange("p (h n) -> p h n", n=KEYS)
                p.tensor_tensor(p8, p8, mul2[:, bass.ds(tile, 1), :].to_broadcast([P, HG, KEYS]), ALU.mult).then_inc(done["maskmul"], 1)

            def gain(key, lane, tick):
                pool.wait_ge(done["norm"], tick.done("norm", "2", lane))
                pool.sem_inc(passed["pool"], 1)
                p.tensor_tensor(x[:, lane, :], z[:, lane, :], rows["g2"][:, :], ALU.mult).then_inc(done["gain"], 1)

            def offset(key, lane, tick):
                pool.wait_ge(done["gain"], tick.done("gain", "2", lane))
                pool.sem_inc(passed["pool"], 1)
                p.tensor_tensor(x[:, lane, :], x[:, lane, :], rows["be2"][:, :], ALU.add).then_inc(done["offset"], 1)

            steps = {"vareps": vareps, "rstd": do_rstd, "prebias": prebias, "keep": keep, "state": state, "maskmul": maskmul,
                     "gain": gain, "offset": offset}
            with pool.Fori(0, PAIRS) as pair:
                tables(pair)
                pool.wait_ge(x_in, (pair + 1) * PAIR * 16)
                pool.sem_inc(passed["pool"], 1)
                with pool.Fori(0, ITERS) as i:
                    tick = counts.tick(0, pair, i)
                    for s, key, lane in counts.order[0]["gpsimd"]:
                        steps[s](key, lane, tick)
                pool.wait_ge(states_set, pair + 1)
                pool.sem_inc(passed["pool"], 1)
                with pool.Fori(0, ITERS) as i:
                    tick = counts.tick(1, pair, i)
                    for s, key, lane in counts.order[1]["gpsimd"]:
                        steps[s](key, lane, tick)


_UNUSED = ["itok_BxS2_4_31999"]


def kernel(**inputs):
    import numpy as _np
    import concourse.bacc as _bacc
    from concourse import mybir as _mybir
    from concourse.bass_utils import run_bass_kernel_spmd as _run

    nc = _bacc.Bacc("TRN2", target_bir_lowering=False, num_devices=1)
    arrays, args = {}, {}
    for name in inputs:
        if name in _UNUSED:
            continue
        a = _np.ascontiguousarray(inputs[name])
        arrays[f"in_{name}_dram"] = a
        args[name] = nc.dram_tensor(f"in_{name}_dram", a.shape, _mybir.dt.from_np(a.dtype), kind="ExternalInput").ap()
    shape = inputs["x"].shape
    args["out"] = nc.dram_tensor("out_0_dram", shape, _mybir.dt.float32, kind="ExternalOutput").ap()
    xattn_chain(nc, args)
    r = _run(nc, [arrays], core_ids=[0])
    return r.results[0]["out_0_dram"]
```
